# Optimizing a Trainium2 kernel written in Bass

```python
import numpy as np
import jax
import jax.numpy as jnp

def _softmax(x, axis=-1):
    return jax.nn.softmax(x, axis=axis)
def _gelu(x):
    return jax.nn.gelu(x, approximate=True)
def _silu(x):
    return jax.nn.silu(x)
def _sigmoid(x):
    return jax.nn.sigmoid(x)
def _layernorm(x, axis=-1, eps=1e-5):
    m = jnp.mean(x, axis=axis, keepdims=True)
    v = jnp.var(x, axis=axis, keepdims=True)
    return (x - m) / jnp.sqrt(v + eps)
def _scatter_add(tgt, idx, src, axis=0):
    return tgt.at[idx].add(src)
def _segment_sum(src, seg, n):
    return jax.ops.segment_sum(src, seg, n)

kernel_name = 'mk_adj_preln_d4_adj_256_8938bb'

def setup_inputs(seed: int = 0):
    np.random.seed(seed)
    _w = jnp.asarray
    def _rec_inputs():
        import jax
        import jax.numpy as jnp
        _gk = jax.random.key(seed)
        x = -0.0002928 + 1 * jax.random.normal(jax.random.fold_in(_gk, 1), (64, 256, 256), jnp.float32)
        _a = jax.random.bernoulli(jax.random.fold_in(_gk, 2), 0.125, (256, 256))
        _a = jnp.logical_or(_a, jnp.swapaxes(_a, -1, -2))
        _a = jnp.logical_or(_a, jnp.eye(256, dtype=bool))
        adj = _a.astype(jnp.int32)
        return x, adj
    x, adj = _rec_inputs()
    def _L0_gnn_setup():
        import jax, jax.numpy as jnp
        import numpy as np
        IN_F = 256
        OUT_F = 256
        ALPHA = 0.01
        NEG_INF = -1000000000.0
        key = jax.random.key(seed)
        k_inp, k_adj, k_W, k_a = jax.random.split(key, 4)
        inp = jax.random.normal(k_inp, (8, 2048, IN_F), dtype=jnp.float32)
        adj = jax.random.randint(k_adj, (2048, 2048), 0, 2, dtype=jnp.int32)
        gain = 1.414
        lim_W = gain * np.sqrt(6.0 / (IN_F + OUT_F))
        W = jax.random.uniform(k_W, (IN_F, OUT_F), minval=-lim_W, maxval=lim_W, dtype=jnp.float32)
        lim_a = gain * np.sqrt(6.0 / (2 * OUT_F + 1))
        a = jax.random.uniform(k_a, (2 * OUT_F, 1), minval=-lim_a, maxval=lim_a, dtype=jnp.float32)
        return {'inp': inp, 'adj': adj, 'W': W, 'a': a}
    _L0_gnn_all = _L0_gnn_setup()
    _L0_gnn_in = {k: v for k, v in _L0_gnn_all.items() if k in ('W', 'a', )}
    del _L0_gnn_all

    def _L1_gnn_setup():
        import jax, jax.numpy as jnp
        import numpy as np
        ALPHA = 0.2
        NEG_INF = -9000000000000000.0

        def _gat(inp, adj_mask, W, a):
            h = jnp.matmul(inp, W)
            F_ = h.shape[-1]
            f1 = jnp.matmul(h, a[:F_, 0])
            f2 = jnp.matmul(h, a[F_:, 0])
            e = jax.nn.leaky_relu(f1[:, :, None] + f2[:, None, :], ALPHA)
            if adj_mask is not None:
                e = jnp.where(adj_mask[None, :, :] > 0, e, NEG_INF)
            att = jax.nn.softmax(e, axis=2)
            h_prime = jnp.einsum('bij,bjf->bif', att, h)
            return jax.nn.elu(h_prime)
        key = jax.random.key(seed)
        ks = jax.random.split(key, 10)
        B, N, Fin, H, O = (16, 1024, 256, 512, 256)

        def xavier(k, shape):
            fan_in, fan_out = (shape[0], shape[-1])
            bound = 1.414 * np.sqrt(6.0 / (fan_in + fan_out))
            return jax.random.uniform(k, shape, jnp.float32, -bound, bound)
        return {'x': jax.random.normal(ks[0], (B, N, Fin), jnp.float32), 'adj': jax.random.randint(ks[1], (N, N), 0, 2, jnp.int32), 'mlp1_w': xavier(ks[2], (Fin, H)), 'mlp1_b': jnp.zeros((H,), jnp.float32), 'mlp2_w': xavier(ks[3], (H, O)), 'mlp2_b': jnp.zeros((O,), jnp.float32), 'W_fc': xavier(ks[4], (H, H)), 'a_fc': xavier(ks[5], (2 * H, 1)), 'W_hand': xavier(ks[6], (O, O)), 'a_hand': xavier(ks[7], (2 * O, 1))}
    _L1_gnn_all = _L1_gnn_setup()
    _L1_gnn_in = {k: v for k, v in _L1_gnn_all.items() if k in ('mlp1_w', 'mlp1_b', 'mlp2_w', 'mlp2_b', 'W_fc', 'a_fc', 'W_hand', 'a_hand', )}
    del _L1_gnn_all

    def _L2_gnn_setup():
        import jax, jax.numpy as jnp
        import numpy as np
        ALPHA = 0.2
        key = jax.random.key(seed)
        k1, k2, k3, k4 = jax.random.split(key, 4)
        B, N, Din, Dout = (8, 2048, 256, 256)
        h = jax.random.normal(k1, (B, N, Din), dtype=jnp.float32)
        adj = jax.random.randint(k2, (N, N), 0, 2, dtype=jnp.int32)
        w_bound = float(np.sqrt(6.0 / (Din + Dout)))
        a_bound = float(np.sqrt(6.0 / (2 * Dout + 1)))
        W = jax.random.uniform(k3, (Din, Dout), dtype=jnp.float32, minval=-w_bound, maxval=w_bound)
        a = jax.random.uniform(k4, (2 * Dout, 1), dtype=jnp.float32, minval=-a_bound, maxval=a_bound)
        return {'h': h, 'adj': adj, 'W': W, 'a': a}
    _L2_gnn_all = _L2_gnn_setup()
    _L2_gnn_in = {k: v for k, v in _L2_gnn_all.items() if k in ('W', 'a', )}
    del _L2_gnn_all

    def _L3_gnn_setup():
        import jax, jax.numpy as jnp
        import numpy as np
        IN_F = 256
        OUT_F = 256
        N_HEADS = 4
        HEAD_DIM = OUT_F // N_HEADS
        B, N = (8, 2048)
        LN_EPS = 1e-05
        key = jax.random.key(seed)
        ks = jax.random.split(key, 12)
        x = jax.random.normal(ks[0], (B, N, IN_F), dtype=jnp.float32)
        adj = jax.random.randint(ks[1], (N, N), 0, 2, dtype=jnp.int32)
        adj = adj.at[jnp.arange(N), jnp.arange(N)].set(1)
        s = 0.02
        Wq = jax.random.normal(ks[2], (IN_F, OUT_F), jnp.float32) * s
        bq = jnp.zeros((OUT_F,), jnp.float32)
        Wk = jax.random.normal(ks[3], (IN_F, OUT_F), jnp.float32) * s
        bk = jnp.zeros((OUT_F,), jnp.float32)
        Wv = jax.random.normal(ks[4], (IN_F, OUT_F), jnp.float32) * s
        bv = jnp.zeros((OUT_F,), jnp.float32)
        Wo = jax.random.normal(ks[5], (OUT_F, OUT_F), jnp.float32) * s
        bo = jnp.zeros((OUT_F,), jnp.float32)
        gamma = jnp.ones((OUT_F,), jnp.float32)
        beta = jnp.zeros((OUT_F,), jnp.float32)
        return {'x': x, 'adj': adj, 'Wq': Wq, 'bq': bq, 'Wk': Wk, 'bk': bk, 'Wv': Wv, 'bv': bv, 'Wo': Wo, 'bo': bo, 'gamma': gamma, 'beta': beta}
    _L3_gnn_all = _L3_gnn_setup()
    _L3_gnn_in = {k: v for k, v in _L3_gnn_all.items() if k in ('Wq', 'bq', 'Wk', 'bk', 'Wv', 'bv', 'Wo', 'bo', 'gamma', 'beta', )}
    del _L3_gnn_all

    return {
        "x": x,
        "adj": adj,
        "L0_gnn_W": _L0_gnn_in["W"],
        "L0_gnn_a": _L0_gnn_in["a"],
        "L1_gnn_mlp1_w": _L1_gnn_in["mlp1_w"],
        "L1_gnn_mlp1_b": _L1_gnn_in["mlp1_b"],
        "L1_gnn_mlp2_w": _L1_gnn_in["mlp2_w"],
        "L1_gnn_mlp2_b": _L1_gnn_in["mlp2_b"],
        "L1_gnn_W_fc": _L1_gnn_in["W_fc"],
        "L1_gnn_a_fc": _L1_gnn_in["a_fc"],
        "L1_gnn_W_hand": _L1_gnn_in["W_hand"],
        "L1_gnn_a_hand": _L1_gnn_in["a_hand"],
        "L2_gnn_W": _L2_gnn_in["W"],
        "L2_gnn_a": _L2_gnn_in["a"],
        "L3_gnn_Wq": _L3_gnn_in["Wq"],
        "L3_gnn_bq": _L3_gnn_in["bq"],
        "L3_gnn_Wk": _L3_gnn_in["Wk"],
        "L3_gnn_bk": _L3_gnn_in["bk"],
        "L3_gnn_Wv": _L3_gnn_in["Wv"],
        "L3_gnn_bv": _L3_gnn_in["bv"],
        "L3_gnn_Wo": _L3_gnn_in["Wo"],
        "L3_gnn_bo": _L3_gnn_in["bo"],
        "L3_gnn_gamma": _L3_gnn_in["gamma"],
        "L3_gnn_beta": _L3_gnn_in["beta"],
    }

def reference(x, adj, L0_gnn_W, L0_gnn_a, L1_gnn_mlp1_w, L1_gnn_mlp1_b, L1_gnn_mlp2_w, L1_gnn_mlp2_b, L1_gnn_W_fc, L1_gnn_a_fc, L1_gnn_W_hand, L1_gnn_a_hand, L2_gnn_W, L2_gnn_a, L3_gnn_Wq, L3_gnn_bq, L3_gnn_Wk, L3_gnn_bk, L3_gnn_Wv, L3_gnn_bv, L3_gnn_Wo, L3_gnn_bo, L3_gnn_gamma, L3_gnn_beta):
    import jax
    import jax.numpy as jnp
    def _L0_gnn_ref(inp, adj, W, a):
        import jax, jax.numpy as jnp
        import numpy as np
        IN_F = 256
        OUT_F = 256
        ALPHA = 0.01
        NEG_INF = -1000000000.0
        h = jnp.matmul(inp, W)
        a1 = a[:OUT_F, 0]
        a2 = a[OUT_F:, 0]
        e_src = jnp.einsum('bnf,f->bn', h, a1)
        e_dst = jnp.einsum('bnf,f->bn', h, a2)
        e = jax.nn.leaky_relu(e_src[:, :, None] + e_dst[:, None, :], negative_slope=ALPHA)
        e = jnp.where(adj[None, :, :] == 0, NEG_INF, e)
        attention = jax.nn.softmax(e, axis=-1)
        h_prime = jnp.matmul(attention, h)
        return jax.nn.relu(h_prime)

    def _L1_gnn_ref(x, adj, mlp1_w, mlp1_b, mlp2_w, mlp2_b, W_fc, a_fc, W_hand, a_hand):
        import jax, jax.numpy as jnp
        import numpy as np
        ALPHA = 0.2
        NEG_INF = -9000000000000000.0

        def _gat(inp, adj_mask, W, a):
            h = jnp.matmul(inp, W)
            F_ = h.shape[-1]
            f1 = jnp.matmul(h, a[:F_, 0])
            f2 = jnp.matmul(h, a[F_:, 0])
            e = jax.nn.leaky_relu(f1[:, :, None] + f2[:, None, :], ALPHA)
            if adj_mask is not None:
                e = jnp.where(adj_mask[None, :, :] > 0, e, NEG_INF)
            att = jax.nn.softmax(e, axis=2)
            h_prime = jnp.einsum('bij,bjf->bif', att, h)
            return jax.nn.elu(h_prime)
        out = jax.nn.relu(jnp.matmul(x, mlp1_w) + mlp1_b)
        residual = out
        out = _gat(jax.nn.relu(out), None, W_fc, a_fc)
        out = jax.nn.elu(out) + residual
        out = jax.nn.relu(jnp.matmul(out, mlp2_w) + mlp2_b)
        residual = out
        out = _gat(jax.nn.relu(out), adj, W_hand, a_hand)
        out = jax.nn.elu(out) + residual
        return jax.nn.relu(out)

    def _L2_gnn_ref(h, adj, W, a):
        import jax, jax.numpy as jnp
        import numpy as np
        ALPHA = 0.2
        Wh = jnp.matmul(h, W)
        D = W.shape[1]
        e_src = jnp.matmul(Wh, a[:D])
        e_dst = jnp.matmul(Wh, a[D:])
        e = e_src + jnp.swapaxes(e_dst, 1, 2)
        e = jnp.where(e > 0, e, ALPHA * e)
        mask = (adj > 0)[None, :, :]
        e = jnp.where(mask, e, -jnp.inf)
        alpha_w = jax.nn.softmax(e, axis=-1)
        h_prime = jnp.matmul(alpha_w, Wh)
        return jax.nn.elu(h_prime)

    def _L3_gnn_ref(x, adj, Wq, bq, Wk, bk, Wv, bv, Wo, bo, gamma, beta):
        import jax, jax.numpy as jnp
        import numpy as np
        IN_F = 256
        OUT_F = 256
        N_HEADS = 4
        HEAD_DIM = OUT_F // N_HEADS
        B, N = (8, 2048)
        LN_EPS = 1e-05
        b, n, _ = x.shape
        Q = (x @ Wq + bq).reshape(b, n, N_HEADS, HEAD_DIM)
        K = (x @ Wk + bk).reshape(b, n, N_HEADS, HEAD_DIM)
        V = (x @ Wv + bv).reshape(b, n, N_HEADS, HEAD_DIM)
        scale = 1.0 / np.sqrt(HEAD_DIM).astype(np.float32)
        scores = jnp.einsum('bnhd,bmhd->bhnm', Q, K) * scale
        mask = (adj == 0)[None, None, :, :]
        scores = jnp.where(mask, -jnp.inf, scores)
        attn = jax.nn.softmax(scores, axis=-1)
        out = jnp.einsum('bhnm,bmhd->bnhd', attn, V).reshape(b, n, OUT_F)
        out = out @ Wo + bo
        mu = jnp.mean(out, axis=-1, keepdims=True)
        var = jnp.mean(jnp.square(out - mu), axis=-1, keepdims=True)
        out = (out - mu) / jnp.sqrt(var + LN_EPS) * gamma + beta
        return out

    h = jnp.maximum(_layernorm(x, axis=-1), 0.0)
    x = x + _L0_gnn_ref(h, adj, L0_gnn_W, L0_gnn_a)
    h = jnp.maximum(_layernorm(x, axis=-1), 0.0)
    x = x + _L1_gnn_ref(h, adj, L1_gnn_mlp1_w, L1_gnn_mlp1_b, L1_gnn_mlp2_w, L1_gnn_mlp2_b, L1_gnn_W_fc, L1_gnn_a_fc, L1_gnn_W_hand, L1_gnn_a_hand)
    h = jnp.maximum(_layernorm(x, axis=-1), 0.0)
    x = x + _L2_gnn_ref(h, adj, L2_gnn_W, L2_gnn_a)
    h = jnp.maximum(_layernorm(x, axis=-1), 0.0)
    x = x + _L3_gnn_ref(h, adj, L3_gnn_Wq, L3_gnn_bq, L3_gnn_Wk, L3_gnn_bk, L3_gnn_Wv, L3_gnn_bv, L3_gnn_Wo, L3_gnn_bo, L3_gnn_gamma, L3_gnn_beta)
    return x


_drawn_inputs = setup_inputs


def setup_inputs(seed=0):
    import zlib

    import numpy as np

    out = dict(_drawn_inputs(seed))
    spreads = {'L1_gnn_mlp1_b': (0.0, 0.1),
     'L1_gnn_mlp2_b': (0.0, 0.1),
     'L3_gnn_bq': (0.0, 0.8),
     'L3_gnn_bk': (0.0, 0.8),
     'L3_gnn_bv': (0.0, 0.1),
     'L3_gnn_bo': (0.0, 0.1),
     'L3_gnn_gamma': (1.0, 0.2),
     'L3_gnn_beta': (0.0, 0.1)}
    factors = {'L1_gnn_a_hand': 6.918, 'L2_gnn_a': 6.306, 'L3_gnn_Wq': 8.0, 'L3_gnn_Wk': 8.0}
    for name, (base, spread) in spreads.items():
        noise = np.random.default_rng([zlib.crc32(name.encode()), seed]).standard_normal(out[name].shape)
        drawn = base * np.exp(spread * noise) if base else spread * noise
        out[name] = jnp.asarray(drawn.astype(out[name].dtype))
    for name, factor in factors.items():
        out[name] = (out[name] * factor).astype(out[name].dtype)
    return out
```

```python
from contextlib import ExitStack

import concourse.bass as bass
from concourse import mybir

ALU = mybir.AluOpType
ACT = mybir.ActivationFunctionType
AX = mybir.AxisListType
F32 = mybir.dt.float32
I32 = mybir.dt.int32

P = 128
LANES = 4
MASKED = -1.0e30
LEAST = -3.0e38
EPS = 1e-5

STEPS = [
    ("stats", 0), ("turn", 0), ("project", 0), ("spread", 0), ("weigh", 0), ("turn_probs", 0), ("mix", 0),
    ("stats", 1), ("turn", 1), ("up", 0), ("full_coefs", 0), ("full_scores", 0), ("weigh", 3), ("turn_full", 0),
    ("mix_full", 0), ("elu_full", 0), ("down", 0),
    ("project", 1), ("spread", 1), ("weigh", 1), ("turn_probs", 1), ("mix", 1), ("finish", 1),
    ("stats", 2), ("turn", 2), ("project", 2), ("spread", 2), ("weigh", 2), ("turn_probs", 2), ("mix", 2), ("finish", 2),
    ("stats", 3), ("turn", 3), ("queries_keys", 0), ("values", 0),
    ("scores", 0), ("scores", 1), ("turn_heads", 0), ("turn_heads", 1),
    ("mix_heads", 0), ("turn_heads_out", 0), ("out_project", 0), ("stats", 4), ("out", 0),
]


def bass_graph_layers(nc, x, adj, W0, a0, mlp1_w, mlp1_b, mlp2_w, mlp2_b, W_fc, a_fc, W_hand, a_hand,
                      W2, a2, Wq, bq, Wk, bk, Wv, bv, Wo, bo, gamma, beta, y):
    SAMPLES, NODES, F = x.shape
    H = mlp1_w.shape[1]
    T = NODES // P
    KT = F // P
    HT = H // P
    HEADS, HD = 4, F // 4
    ROUNDS = SAMPLES // LANES
    SLOPE = [0.01, 0.2, 0.2]
    FULL_SLOPE = 0.2
    SCALE = 1.0 / float(HD) ** 0.5
    assert T == 2 and KT == 2 and HT == 4 and SAMPLES % LANES == 0 and ROUNDS >= 3

    def turns():
        found = []
        for slot in range(len(STEPS)):
            for lane in range(LANES):
                k = slot - lane * len(STEPS) // LANES
                found.append((k < 0, lane, STEPS[k % len(STEPS)]))
        return [(step, lane, late) for late, lane, step in found]

    TURNS = turns()

    with ExitStack() as ctx:
        def sb(name, shape, dt=F32):
            return ctx.enter_context(nc.sbuf_tensor(name, shape, dt))

        def sem(name):
            return ctx.enter_context(nc.semaphore(name))

        def sems(name, n):
            return [sem(f"{name}{i}") for i in range(n)]

        w_gat = [sb(f"w_gat{g}", [P, KT, F + 2]) for g in range(3)]
        w_up = sb("w_up", [P, KT, H])
        w_full = sb("w_full", [P, HT, H])
        w_full_a = sb("w_full_a", [P, HT, 2])
        w_down = sb("w_down", [P, HT, F])
        w_q, w_k, w_v, w_o = (sb(n, [P, KT, F]) for n in ("w_q", "w_k", "w_v", "w_o"))
        b_up = sb("b_up", [P, HT])
        b_down, b_q, b_k = (sb(n, [P, KT]) for n in ("b_down", "b_q", "b_k"))
        b_v, b_o, gamma_b, beta_b = (sb(n, [P, F]) for n in ("b_v", "b_o", "gamma_b", "beta_b"))
        mask_zero = sb("mask_zero", [P, T, NODES])
        mask_neg = sb("mask_neg", [P, T, NODES])
        masks = [mask_zero, mask_neg, mask_neg]
        ident = sb("ident", [P, P])
        minus_one = sb("minus_one", [P, 1])
        minus_half = sb("minus_half", [P, T])
        eps = sb("eps", [P, T])

        def lanes(name, shape):
            return [sb(f"{name}{s}", shape) for s in range(LANES)]

        x_in = lanes("x_in", [P, T, F])
        x_cur = lanes("x_cur", [P, T, F])
        y_out = lanes("y_out", [P, T, F])
        norm = lanes("norm", [P, T, F])
        norm_t = lanes("norm_t", [P, KT, NODES])
        h_buf = lanes("h_buf", [P, T * H])
        hid_t = lanes("hid_t", [P, HT, NODES])
        low_t = lanes("low_t", [P, KT, NODES])
        probs = lanes("probs", [P, HEADS, T, NODES])
        probs_t = lanes("probs_t", [P, HEADS, T, NODES])
        stat = lanes("stat", [P, T, 6])
        mean_var = lanes("mean_var", [P, T, 2])
        var_eps = lanes("var_eps", [P, T])
        rstd = lanes("rstd", [P, T])
        top = lanes("top", [P, HEADS, T])
        neg_top = lanes("neg_top", [P, HEADS, T])
        shift = lanes("shift", [P, HEADS, T])
        sums = lanes("sums", [P, HEADS, T])
        inv = lanes("inv", [P, HEADS, T])
        coefs = lanes("coefs", [P, T, 2])
        h_wide = [b[:, :].rearrange("p (t f) -> p t f", t=T) for b in h_buf]
        h_gat = [b[:, 0:T * (F + 2)].rearrange("p (t f) -> p t f", t=T) for b in h_buf]
        vals = [b[:, 0:T * F].rearrange("p (t f) -> p t f", t=T) for b in h_buf]
        q_t = [b[:, 0:KT, :] for b in hid_t]
        k_t = [b[:, KT:2 * KT, :] for b in hid_t]
        att, att_t, out_pre = norm, low_t, norm
        pair = [ctx.enter_context(nc.psum_tensor(f"banks{s}", [P, 2, 512], F32)) for s in range(LANES)]
        banks = [[b[:, i, :] for i in range(2)] for b in pair]
        setup_adj = probs[0][:, 0, :, :].bitcast(I32)
        setup_a = probs_t[0][:, :, :, :].rearrange("p h t n -> p (h t n)")
        setup_junk = probs[1][:, 0, :, :].rearrange("p t n -> p (t n)")

        def wide(ap):
            return ap[:, :, :].rearrange("p t f -> p (t f)")

        def pair_of(buf, i):
            return buf[:, 2 * i:2 * i + 2, :, :].rearrange("p h t n -> p (h t n)")

        s_adj, s_avec, s_weights = sem("s_adj"), sem("s_avec"), sem("s_weights")
        s_ident, s_const, s_folded = sem("s_ident"), sem("s_const"), sem("s_folded")
        x_loaded, y_stored = sems("x_loaded", LANES), sems("y_stored", LANES)
        stats_made, var_ready, eps_added, rstd_ready, normed = (
            sems(n, 5) for n in ("stats_made", "var_ready", "eps_added", "rstd_ready", "normed"))
        turned, norm_t_ready = sems("turned", 4), sems("norm_t_ready", 4)
        h_mm, h_ready = sems("h_mm", 3), sems("h_ready", 3)
        spreaded, top_ready, neg_top_ready, shift_ready, scores_ready, leaky_ready, exps_ready, inv_ready, probs_ready, \
            probs_turned, probs_t_ready = (sems(n, 4) for n in (
                "spreaded", "top_ready", "neg_top_ready", "shift_ready", "scores_ready", "leaky_ready", "exps_ready", "inv_ready",
                "probs_ready", "probs_turned", "probs_t_ready"))
        mixed, x_updated = sems("mixed", 3), sems("x_updated", 3)
        low_ready, exp_low_ready, elu_ready = (
            [None] + sems(n, 2) for n in ("low_ready", "exp_low_ready", "elu_ready"))
        exp_exp_ready, sum_ready = sem("exp_exp_ready"), sem("sum_ready")
        up_mm, hid_ready, coefs_mm, coefs_ready = (
            sem(n) for n in ("up_mm", "hid_ready", "coefs_mm", "coefs_ready"))
        full_mm, full_ready = sems("full_mm", 2), sems("full_ready", 2)
        full_mixed, full_low, full_exp, full_exp_exp, full_elu, full_sum = (
            sem(n) for n in ("full_mixed", "full_low", "full_exp", "full_exp_exp", "full_elu", "full_sum"))
        down_mm, low_t_ready = sem("down_mm"), sem("low_t_ready")
        qk_mm, v_mm, q_ready, k_ready, v_ready = (sem(n) for n in ("qk_mm", "v_mm", "q_ready", "k_ready", "v_ready"))
        score_mm, head_top, head_shift, head_exps, head_turned, head_t_ready = (
            sems(n, HEADS // 2) for n in ("score_mm", "head_top", "head_shift", "head_exps", "head_turned",
                                          "head_t_ready"))
        av_mm, head_inv, att_ready, att_turned, att_t_ready = (
            sem(n) for n in ("av_mm", "head_inv", "att_ready", "att_turned", "att_t_ready"))
        wo_mm, out_pre_ready, x_beta_ready, scaled_ready, y_ready = (
            sem(n) for n in ("wo_mm", "out_pre_ready", "x_beta_ready", "scaled_ready", "y_ready"))

        x_d = x.rearrange("b (p t) f -> b p t f", t=T)
        y_d = y.rearrange("b (p t) f -> b p t f", t=T)

        def rows(w):
            return w.rearrange("(k p) f -> p k f", p=P)

        def column(b):
            return b.rearrange("(k p) -> p k", p=P)

        def everywhere(v):
            return v.rearrange("(o f) -> o f", o=1).to_broadcast([P, v.shape[0]])

        A_VECS = [(a0, 0), (a_hand, 2 * F), (a2, 4 * F)]
        WEIGHTS = [
            (w_gat[0][:, :, 0:F], rows(W0)), (w_gat[1][:, :, 0:F], rows(W_hand)), (w_gat[2][:, :, 0:F], rows(W2)),
            (w_full[:, :, :], rows(W_fc)),
            (w_up[:, :, :], rows(mlp1_w)), (w_down[:, :, :], rows(mlp2_w)),
            (w_q[:, :, :], rows(Wq)), (w_k[:, :, :], rows(Wk)), (w_v[:, :, :], rows(Wv)), (w_o[:, :, :], rows(Wo)),
            (b_up[:, :], column(mlp1_b)), (b_down[:, :], column(mlp2_b)), (b_q[:, :], column(bq)),
            (b_k[:, :], column(bk)),
            (b_v[:, :], everywhere(bv)), (b_o[:, :], everywhere(bo)), (gamma_b[:, :], everywhere(gamma)),
            (beta_b[:, :], everywhere(beta)),
        ]

        def run(eng, steps, loaded=None):
            for (name, arg), lane, late in TURNS:
                if not late and name in steps:
                    steps[name](arg, lane, lane + 1, 16)
            with eng.Fori(0, ROUNDS - 1) as r:
                n_late = [eng.snap(r * LANES + (s + 1)) for s in range(LANES)]
                n_new = [eng.snap(r * LANES + (LANES + s + 1)) for s in range(LANES)]
                dma_late, dma_new = eng.snap(r * 16 + 16), eng.snap(r * 16 + 32)
                for v in n_late + n_new:
                    eng.to_reg(v)
                for (name, arg), lane, late in TURNS:
                    if name in steps:
                        steps[name](arg, lane, n_late[lane] if late else n_new[lane], dma_late if late else dma_new)
            for (name, arg), lane, late in TURNS:
                if late and name in steps:
                    steps[name](arg, lane, (ROUNDS - 1) * LANES + lane + 1, 16 * ROUNDS)

        block = ctx.enter_context(nc.Block())

        @block.sync
        def _(sp):
            sp.dma_start(setup_adj, adj.rearrange("(p t) j -> p t j", t=T)).then_inc(s_adj, 16)
            sp.dma_start(setup_a[:, 0:2 * F], everywhere(a0.rearrange("f o -> (f o)"))).then_inc(s_avec, 16)
            sp.dma_start(setup_a[:, 2 * F:4 * F], everywhere(a_hand.rearrange("f o -> (f o)"))).then_inc(s_avec, 16)
            sp.dma_start(setup_a[:, 4 * F:6 * F], everywhere(a2.rearrange("f o -> (f o)"))).then_inc(s_avec, 16)
            sp.dma_start(x_in[0][:, :, :], x_d[0]).then_inc(x_loaded[0], 16)
            with nc.allow_non_contiguous_dma(reason="four bias vectors, once"):
                for dst, src in WEIGHTS:
                    sp.dma_start(dst, src).then_inc(s_weights, 16)
            sp.wait_ge(s_folded, 6 * KT)
            sp.dma_start(setup_a[:, 0:2 * H], everywhere(a_fc.rearrange("f o -> (f o)"))).then_inc(s_avec, 16)
            for s in range(LANES):
                sp.sem_inc(y_stored[s], 16)
            for s in range(1, LANES):
                sp.dma_start(x_in[s][:, :, :], x_d[s]).then_inc(x_loaded[s], 16)
            for s in range(LANES):
                sp.wait_ge(x_updated[0], s + 1)
                sp.dma_start(x_in[s][:, :, :], x_d[LANES + s]).then_inc(x_loaded[s], 16)
            with sp.Fori(0, ROUNDS - 2) as r:
                for s in range(LANES):
                    sp.wait_ge(x_updated[0], r * LANES + (LANES + s + 1))
                    sp.dma_start(x_in[s][:, :, :], x_d[r * LANES + (2 * LANES + s)]).then_inc(x_loaded[s], 16)
                    sp.wait_ge(y_ready, r * LANES + (s + 1))
                    sp.dma_start(y_d[r * LANES + s], y_out[s][:, :, :]).then_inc(y_stored[s], 16)
            for n in range((ROUNDS - 2) * LANES, SAMPLES):
                sp.wait_ge(y_ready, n + 1)
                sp.dma_start(y_d[n], y_out[n % LANES][:, :, :]).then_inc(y_stored[n % LANES], 16)
            for s in range(LANES):
                sp.wait_ge(y_stored[s], 16 * (ROUNDS + 1))

        @block.gpsimd
        def _(pool):
            pool.memset(ident[:, :], 0.0).then_inc(s_ident, 1)
            pool.memset(minus_one[:, :], -1.0).then_inc(s_const, 1)
            pool.memset(minus_half[:, :], -0.5).then_inc(s_const, 1)
            pool.memset(eps[:, :], EPS).then_inc(s_const, 1)
            pool.wait_ge(s_ident, 1)
            pool.affine_select(out=ident[:, :], in_=ident[:, :], compare_op=ALU.not_equal, fill=1.0, base=0,
                               pattern=[[-1, P]], channel_multiplier=1).then_inc(s_ident, 1)
            pool.wait_ge(s_const, 3)
            pool.wait_ge(s_weights, 16 * len(WEIGHTS))

            def stats(l, s, n, dma):
                pool.wait_ge(var_ready[l], n)
                pool.tensor_tensor(var_eps[s][:, :], mean_var[s][:, :, 1], eps[:, :], ALU.add)\
                    .then_inc(eps_added[l], 1)
                pool.wait_ge(eps_added[l], n)
                pool.tensor_tensor(rstd[s][:, :], var_eps[s][:, :], minus_half[:, :], ALU.pow)\
                    .then_inc(rstd_ready[l], 1)

            def elu_full(_, s, n, dma):
                pool.wait_ge(full_elu, n)
                pool.tensor_tensor(wide(hid_t[s]), wide(hid_t[s]), pair_of(probs_t[s], 1), ALU.add)\
                    .then_inc(full_sum, 1)

            def finish(g, s, n, dma):
                if g == 2:
                    pool.wait_ge(elu_ready[2], n)
                    pool.tensor_tensor(x_cur[s][:, :, :], x_cur[s][:, :, :], probs[s][:, 1, :, :], ALU.add)\
                        .then_inc(x_updated[2], 1)

            def values(_, s, n, dma):
                pool.wait_ge(normed[3], n)
                pool.tensor_tensor(x_cur[s][:, :, :], x_cur[s][:, :, :],
                                   beta_b[:, :].unsqueeze(1).to_broadcast([P, T, F]), ALU.add)\
                    .then_inc(x_beta_ready, 1)

            def out(_, s, n, dma):
                pool.wait_ge(normed[4], n)
                pool.tensor_tensor(norm[s][:, :, :], norm[s][:, :, :],
                                   gamma_b[:, :].unsqueeze(1).to_broadcast([P, T, F]), ALU.mult)\
                    .then_inc(scaled_ready, 1)
                pool.wait_ge(scaled_ready, n)
                pool.wait_ge(x_beta_ready, n)
                pool.wait_ge(y_stored[s], dma)
                pool.tensor_tensor(y_out[s][:, :, :], norm[s][:, :, :], x_cur[s][:, :, :], ALU.add)\
                    .then_inc(y_ready, 1)

            run(pool, {"stats": stats, "elu_full": elu_full, "finish": finish, "values": values, "out": out})

        @block.scalar
        def _(act):
            act.preload_act_table(ACT.Exp)
            act.wait_ge(s_const, 3)
            act.wait_ge(s_weights, 16 * len(WEIGHTS))
            act.wait_ge(s_folded, 6 * KT + 2 * HT)

            def turn(l, s, n, dma):
                act.wait_ge(turned[l], n)
                act.activation(wide(norm_t[s]), banks[s][0][:, :], ACT.Relu).then_inc(norm_t_ready[l], 1)

            def project(g, s, n, dma):
                act.wait_ge(h_mm[g], n)
                act.activation(h_gat[s], pair[s][:, :, 0:F + 2], ACT.Copy).then_inc(h_ready[g], 1)

            def add_f1(g, s, n, src, column_of):
                for t in range(T):
                    add = act.activation(probs[s][:, 0, t, :], src(t), ACT.Identity, bias=column_of(t))
                add.then_inc(scores_ready[g], 1)

            def spread(g, s, n, dma):
                act.wait_ge(top_ready[g], n)
                add_f1(g, s, n, lambda t: probs[s][:, 0, t, :], lambda t: h_gat[s][:, t, F:F + 1])

            def weigh(g, s, n, dma):
                act.wait_ge(leaky_ready[g], n)
                act.wait_ge(shift_ready[g], n)
                for t in range(T):
                    ex = act.activation(probs[s][:, 0, t, :], probs[s][:, 0, t, :], ACT.Exp,
                                        bias=shift[s][:, 0, t:t + 1], accum_out=sums[s][:, 0, t:t + 1])
                ex.then_inc(exps_ready[g], 1)

            def turn_probs(g, s, n, dma):
                act.wait_ge(probs_turned[g], n)
                act.activation(wide(probs_t[s][:, 0, :, :]), banks[s][0][:, :], ACT.Copy)\
                    .then_inc(probs_t_ready[g], 1)

            def mix(g, s, n, dma):
                if g == 0:
                    return
                act.wait_ge(low_ready[g], n)
                act.activation(probs[s][:, 2, :, :], probs[s][:, 2, :, :], ACT.Exp).then_inc(exp_low_ready[g], 1)
                if g == 1:
                    act.wait_ge(exp_low_ready[1], n)
                    act.activation(probs[s][:, 2, :, :], probs[s][:, 2, :, :], ACT.Exp, bias=minus_one[:, 0:1])\
                        .then_inc(exp_exp_ready, 1)

            def full_coefs(_, s, n, dma):
                act.wait_ge(full_mm[0], n)
                act.activation(h_wide[s][:, 0, :], banks[s][0][:, :], ACT.Copy).then_inc(full_ready[0], 1)

            def full_scores(_, s, n, dma):
                act.wait_ge(coefs_ready, n)
                act.wait_ge(top_ready[3], n)
                add_f1(3, s, n, lambda t: banks[s][0][:, 0:NODES], lambda t: coefs[s][:, t, 0:1])

            def turn_full(_, s, n, dma):
                act.wait_ge(probs_turned[3], n)
                act.activation(wide(probs_t[s][:, 0, :, :]), banks[s][1][:, :], ACT.Copy)\
                    .then_inc(probs_t_ready[3], 1)

            def mix_full(_, s, n, dma):
                low = pair_of(probs[s], 1)
                act.wait_ge(full_low, n)
                act.activation(low, low, ACT.Exp).then_inc(full_exp, 1)
                act.wait_ge(full_exp, n)
                act.activation(low, low, ACT.Exp, bias=minus_one[:, 0:1]).then_inc(full_exp_exp, 1)

            def down(_, s, n, dma):
                act.wait_ge(down_mm, n)
                for f in range(KT):
                    relu = act.activation(low_t[s][:, f, :], banks[s][0][:, f * NODES:(f + 1) * NODES], ACT.Relu,
                                          bias=b_down[:, f:f + 1])
                relu.then_inc(low_t_ready, 1)

            def queries_keys(_, s, n, dma):
                act.wait_ge(qk_mm, n)
                for f in range(KT):
                    q = act.activation(q_t[s][:, f, :], banks[s][1][:, f * NODES:(f + 1) * NODES], ACT.Identity,
                                       bias=b_q[:, f:f + 1])
                q.then_inc(q_ready, 1)

            def scores(i, s, n, dma):
                act.wait_ge(head_shift[i], n)
                for h in (2 * i, 2 * i + 1):
                    for t in range(T):
                        ex = act.activation(probs[s][:, h, t, :], probs[s][:, h, t, :], ACT.Exp,
                                            bias=shift[s][:, h, t:t + 1], scale=SCALE,
                                            accum_out=sums[s][:, h, t:t + 1])
                ex.then_inc(head_exps[i], 1)

            def turn_heads(i, s, n, dma):
                if i == 0:
                    act.wait_ge(head_turned[0], n)
                    act.activation(pair_of(probs_t[s], 0), wide(pair[s]), ACT.Copy).then_inc(head_t_ready[0], 1)

            def turn_heads_out(_, s, n, dma):
                act.wait_ge(att_turned, n)
                act.activation(wide(att_t[s]), banks[s][1][:, :], ACT.Copy).then_inc(att_t_ready, 1)

            run(act, {"turn": turn, "project": project, "spread": spread, "weigh": weigh, "turn_probs": turn_probs, "mix": mix,
                      "full_coefs": full_coefs, "full_scores": full_scores, "turn_full": turn_full,
                      "mix_full": mix_full, "down": down, "queries_keys": queries_keys, "scores": scores,
                      "turn_heads": turn_heads, "turn_heads_out": turn_heads_out})

        @block.vector
        def _(dve):
            dve.wait_ge(s_weights, 16 * len(WEIGHTS))
            dve.wait_ge(s_adj, 16)
            by_tile = setup_adj.rearrange("p t (q u) -> p t u q", u=T)
            for t in range(T):
                for mask, test in ((mask_zero, ALU.is_equal), (mask_neg, ALU.is_le)):
                    dve.tensor_scalar(mask[:, t, :].rearrange("p (u q) -> p u q", u=T), by_tile[:, t], 0.0, MASKED,
                                      test, ALU.mult).then_inc(s_const, 1)
            dve.wait_ge(s_avec, 48)
            folds = 0
            for g in range(3):
                for k in range(KT):
                    for half in range(2):
                        a = setup_a[:, (2 * g + half) * F:(2 * g + half + 1) * F]
                        if folds:
                            dve.wait_ge(s_folded, folds)
                        dve.tensor_tensor_reduce(setup_junk[:, 0:F], w_gat[g][:, k, 0:F], a, 1.0, 0.0, ALU.mult,
                                                 ALU.add, w_gat[g][:, k, F + half:F + half + 1]).then_inc(s_folded, 1)
                        folds += 1
            dve.wait_ge(s_avec, 64)
            for k in range(HT):
                for half in range(2):
                    dve.wait_ge(s_folded, folds)
                    dve.tensor_tensor_reduce(setup_junk[:, 0:H], w_full[:, k, :], setup_a[:, half * H:(half + 1) * H],
                                             1.0, 0.0, ALU.mult, ALU.add, w_full_a[:, k, half:half + 1])\
                        .then_inc(s_folded, 1)
                    folds += 1
            assert folds == 6 * KT + 2 * HT
            dve.wait_ge(s_folded, folds)
            dve.wait_ge(s_const, 3 + 2 * T)

            def normalise(l, s, n):
                dve.wait_ge(rstd_ready[l], n)
                src = x_in[s] if l == 0 else norm[s] if l == 4 else x_cur[s]
                for t in range(T):
                    nm = dve.tensor_scalar(norm[s][:, t, :], src[:, t, :], mean_var[s][:, t, 0:1],
                                           rstd[s][:, t:t + 1], ALU.subtract, ALU.mult)
                nm.then_inc(normed[l], 1)

            def stats(l, s, n, dma):
                if l == 0:
                    dve.wait_ge(x_loaded[s], dma)
                elif l == 4:
                    dve.wait_ge(out_pre_ready, n)
                else:
                    dve.wait_ge(x_updated[l - 1], n)
                src = x_in[s] if l == 0 else out_pre[s] if l == 4 else x_cur[s]
                for t in range(T):
                    st = dve.bn_stats(stat[s][:, t, :], src[:, t, :])
                st.then_inc(stats_made[l], 1)
                dve.wait_ge(s_const, 3)
                dve.wait_ge(stats_made[l], n)
                for t in range(T):
                    ag = dve.bn_aggr(mean_var[s][:, t, :], stat[s][:, t, :])
                ag.then_inc(var_ready[l], 1)

            def turn(l, s, n, dma):
                normalise(l, s, n)

            def spread(g, s, n, dma):
                dve.wait_ge(s_const, 3)
                dve.wait_ge(spreaded[g], n)
                for t in range(T):
                    tt = dve.tensor_tensor_reduce(probs[s][:, 0, t, :], banks[s][1][:, 0:NODES], masks[g][:, t, :],
                                                  1.0, LEAST, ALU.add, ALU.max, top[s][:, 0, t:t + 1])
                tt.then_inc(top_ready[g], 1)
                dve.wait_ge(top_ready[g], n)
                dve.scalar_tensor_tensor(out=neg_top[s][:, 0, :], in0=top[s][:, 0, :], scalar=-1.0,
                                         in1=h_gat[s][:, :, F], op0=ALU.mult, op1=ALU.subtract)\
                    .then_inc(neg_top_ready[g], 1)
                dve.wait_ge(neg_top_ready[g], n)
                dve.scalar_tensor_tensor(out=shift[s][:, 0, :], in0=neg_top[s][:, 0, :], scalar=SLOPE[g],
                                         in1=neg_top[s][:, 0, :], op0=ALU.mult, op1=ALU.min)\
                    .then_inc(shift_ready[g], 1)

            def weigh(g, s, n, dma):
                slope = (SLOPE + [FULL_SLOPE])[g]
                row = probs[s][:, 0, :, :].rearrange("p t n -> p (t n)")
                dve.wait_ge(scores_ready[g], n)
                dve.scalar_tensor_tensor(out=row, in0=row, scalar=slope, in1=row, op0=ALU.mult, op1=ALU.max)\
                    .then_inc(leaky_ready[g], 1)

            def divide(g, s, n):
                dve.wait_ge(exps_ready[g], n)
                dve.reciprocal(inv[s][:, 0, :], sums[s][:, 0, :]).then_inc(inv_ready[g], 1)
                dve.wait_ge(inv_ready[g], n)
                for t in range(T):
                    pr = dve.tensor_scalar(probs[s][:, 0, t, :], probs[s][:, 0, t, :], inv[s][:, 0, t:t + 1], None,
                                           ALU.mult)
                pr.then_inc(probs_ready[g], 1)

            def turn_probs(g, s, n, dma):
                divide(g, s, n)

            def mix(g, s, n, dma):
                dve.wait_ge(mixed[g], n)
                if g == 0:
                    dve.scalar_tensor_tensor(out=wide(x_cur[s]), in0=banks[s][1][:, :], scalar=0.0,
                                             in1=wide(x_in[s]), op0=ALU.max, op1=ALU.add).then_inc(x_updated[0], 1)
                else:
                    dve.tensor_scalar(wide(probs[s][:, 2, :, :]), banks[s][1][:, :], 0.0, None, ALU.min)\
                        .then_inc(low_ready[g], 1)

            def finish(g, s, n, dma):
                dve.wait_ge(exp_exp_ready if g == 1 else exp_low_ready[2], n)
                dve.scalar_tensor_tensor(out=wide(probs[s][:, 1, :, :]), in0=wide(probs[s][:, 2, :, :]), scalar=-1.0,
                                         in1=banks[s][1][:, :], op0=ALU.add, op1=ALU.max).then_inc(elu_ready[g], 1)
                if g == 1:
                    dve.wait_ge(elu_ready[1], n)
                    dve.tensor_tensor(wide(probs[s][:, 1, :, :]), banks[s][0][:, :], wide(probs[s][:, 1, :, :]),
                                      ALU.add).then_inc(sum_ready, 1)
                    dve.wait_ge(sum_ready, n)
                    dve.scalar_tensor_tensor(out=wide(x_cur[s]), in0=wide(probs[s][:, 1, :, :]), scalar=0.0,
                                             in1=wide(x_cur[s]), op0=ALU.max, op1=ALU.add).then_inc(x_updated[1], 1)

            def up(_, s, n, dma):
                dve.wait_ge(up_mm, n)
                for f in range(HT):
                    relu = dve.tensor_scalar(hid_t[s][:, f, :], banks[s][f // 2][:, (f % 2) * NODES:][:, 0:NODES],
                                             b_up[:, f:f + 1], 0.0, ALU.add, ALU.max)
                relu.then_inc(hid_ready, 1)

            def full_coefs(_, s, n, dma):
                dve.wait_ge(coefs_mm, n)
                dve.tensor_copy(wide(coefs[s]), banks[s][1][:, 0:2 * T]).then_inc(coefs_ready, 1)

            def full_scores(_, s, n, dma):
                dve.wait_ge(spreaded[3], n)
                dve.tensor_reduce(top[s][:, 0, 0:1], banks[s][0][:, 0:NODES], AX.X, ALU.max).then_inc(top_ready[3], 1)
                dve.wait_ge(top_ready[3], n)
                dve.wait_ge(coefs_ready, n)
                dve.tensor_scalar(neg_top[s][:, 0, :], coefs[s][:, :, 0], -1.0, top[s][:, 0, 0:1], ALU.mult,
                                  ALU.subtract).then_inc(neg_top_ready[3], 1)
                dve.wait_ge(neg_top_ready[3], n)
                dve.scalar_tensor_tensor(out=shift[s][:, 0, :], in0=neg_top[s][:, 0, :], scalar=FULL_SLOPE,
                                         in1=neg_top[s][:, 0, :], op0=ALU.mult, op1=ALU.min)\
                    .then_inc(shift_ready[3], 1)
                dve.wait_ge(full_mm[1], n)
                dve.tensor_copy(h_wide[s][:, 1, :], banks[s][1][:, :]).then_inc(full_ready[1], 1)

            def turn_full(_, s, n, dma):
                divide(3, s, n)

            def mix_full(_, s, n, dma):
                dve.wait_ge(full_mixed, n)
                dve.tensor_scalar(pair_of(probs[s], 1), wide(pair[s]), 0.0, None, ALU.min).then_inc(full_low, 1)

            def elu_full(_, s, n, dma):
                dve.wait_ge(full_exp_exp, n)
                dve.scalar_tensor_tensor(out=pair_of(probs_t[s], 1), in0=pair_of(probs[s], 1), scalar=-1.0,
                                         in1=wide(pair[s]), op0=ALU.add, op1=ALU.max).then_inc(full_elu, 1)

            def queries_keys(_, s, n, dma):
                dve.wait_ge(qk_mm, n)
                for f in range(KT):
                    k = dve.tensor_scalar(k_t[s][:, f, :], banks[s][0][:, f * NODES:(f + 1) * NODES], b_k[:, f:f + 1],
                                          None, ALU.add)
                k.then_inc(k_ready, 1)

            def values(_, s, n, dma):
                dve.wait_ge(v_mm, n)
                dve.tensor_tensor(vals[s], banks[s][1][:, :].rearrange("p (t f) -> p t f", t=T),
                                  b_v[:, :].unsqueeze(1).to_broadcast([P, T, F]), ALU.add).then_inc(v_ready, 1)

            def scores(i, s, n, dma):
                dve.wait_ge(s_const, 3)
                dve.wait_ge(score_mm[i], n)
                for h in (2 * i, 2 * i + 1):
                    for t in range(T):
                        tt = dve.tensor_tensor_reduce(probs[s][:, h, t, :],
                                                      banks[s][h % 2][:, t * NODES:(t + 1) * NODES],
                                                      mask_zero[:, t, :], 1.0, LEAST, ALU.add, ALU.max,
                                                      top[s][:, h, t:t + 1])
                tt.then_inc(head_top[i], 1)
                dve.wait_ge(head_top[i], n)
                dve.tensor_scalar(shift[s][:, 2 * i:2 * i + 2, :], top[s][:, 2 * i:2 * i + 2, :], -SCALE, None,
                                  ALU.mult).then_inc(head_shift[i], 1)

            def turn_heads(i, s, n, dma):
                if i == 1:
                    dve.wait_ge(head_turned[1], n)
                    dve.tensor_copy(pair_of(probs_t[s], 1), wide(pair[s])).then_inc(head_t_ready[1], 1)

            def mix_heads(_, s, n, dma):
                dve.wait_ge(head_exps[1], n)
                dve.reciprocal(inv[s][:, :, :], sums[s][:, :, :]).then_inc(head_inv, 1)
                dve.wait_ge(head_inv, n)
                dve.wait_ge(av_mm, n)
                dve.tensor_tensor(att[s][:, :, :].rearrange("p t (h d) -> p t h d", h=HEADS),
                                  banks[s][0][:, :].rearrange("p (t h d) -> p t h d", t=T, h=HEADS),
                                  inv[s][:, :, :].rearrange("p h t -> p t h").unsqueeze(3)
                                  .to_broadcast([P, T, HEADS, HD]), ALU.mult).then_inc(att_ready, 1)

            def out_project(_, s, n, dma):
                dve.wait_ge(wo_mm, n)
                dve.tensor_tensor(out_pre[s][:, :, :], banks[s][0][:, :].rearrange("p (t f) -> p t f", t=T),
                                  b_o[:, :].unsqueeze(1).to_broadcast([P, T, F]), ALU.add)\
                    .then_inc(out_pre_ready, 1)

            def out(_, s, n, dma):
                normalise(4, s, n)

            run(dve, {"stats": stats, "turn": turn, "spread": spread, "weigh": weigh, "turn_probs": turn_probs,
                      "mix": mix, "finish": finish, "up": up, "full_coefs": full_coefs, "full_scores": full_scores,
                      "turn_full": turn_full, "mix_full": mix_full, "elu_full": elu_full,
                      "queries_keys": queries_keys, "values": values, "scores": scores, "turn_heads": turn_heads,
                      "mix_heads": mix_heads, "out_project": out_project, "out": out})

        @block.tensor
        def _(pe):
            pe.wait_ge(s_ident, 2)
            pe.wait_ge(s_weights, 16 * len(WEIGHTS))
            pe.wait_ge(s_folded, 6 * KT + 2 * HT)

            def product(out, lhs, rhs):
                for k, (a, b) in enumerate(zip(lhs, rhs)):
                    mm = pe.matmul(out, a, b, start=(k == 0), stop=(k == len(lhs) - 1))
                return mm

            def turn_tiles(bank, src):
                for a in range(2):
                    for b in range(2):
                        tr = pe.transpose(bank[:, b * 2 * P + a * P:b * 2 * P + (a + 1) * P],
                                          src[:, a, b * P:(b + 1) * P], ident[:, :])
                return tr

            def tile(t):
                return slice(t * P, (t + 1) * P)

            def turn(l, s, n, dma):
                pe.wait_ge(normed[l], n)
                turn_tiles(banks[s][0], norm[s]).then_inc(turned[l], 1)

            def project(g, s, n, dma):
                src = low_t[s] if g == 1 else norm_t[s]
                pe.wait_ge(low_t_ready if g == 1 else norm_t_ready[[0, None, 2][g]], n)
                for t in range(T):
                    mm = product(banks[s][t][:, 0:F + 2], [src[:, k, tile(t)] for k in range(KT)],
                                 [w_gat[g][:, k, :] for k in range(KT)])
                mm.then_inc(h_mm[g], 1)

            def spread(g, s, n, dma):
                pe.wait_ge(h_ready[g], n)
                for t in range(T):
                    tr = pe.transpose(banks[s][1][:, tile(t)], h_gat[s][:, t, F + 1:F + 2].to_broadcast([P, P]),
                                      ident[:, :])
                tr.then_inc(spreaded[g], 1)

            def turn_probs(g, s, n, dma):
                pe.wait_ge(probs_ready[g], n)
                turn_tiles(banks[s][0], probs[s][:, 0, :, :]).then_inc(probs_turned[g], 1)

            def mix(g, s, n, dma):
                pe.wait_ge(probs_t_ready[g], n)
                for t in range(T):
                    mm = product(banks[s][1][:, t * F:(t + 1) * F],
                                 [probs_t[s][:, 0, u, tile(t)] for u in range(T)],
                                 [h_gat[s][:, u, 0:F] for u in range(T)])
                if g == 1:
                    mm = turn_tiles(banks[s][0], low_t[s])
                mm.then_inc(mixed[g], 1)

            def up(_, s, n, dma):
                pe.wait_ge(norm_t_ready[1], n)
                for half in range(2):
                    for f in range(2):
                        mm = product(banks[s][half][:, f * NODES:(f + 1) * NODES],
                                     [w_up[:, k, tile(2 * half + f)] for k in range(KT)],
                                     [norm_t[s][:, k, :] for k in range(KT)])
                mm.then_inc(up_mm, 1)

            def full_rows(t, s, bank):
                return product(bank[:, :], [hid_t[s][:, k, tile(t)] for k in range(HT)],
                               [w_full[:, k, :] for k in range(HT)])

            def full_coefs(_, s, n, dma):
                pe.wait_ge(hid_ready, n)
                for t in range(T):
                    mm = product(banks[s][1][:, 2 * t:2 * t + 2], [hid_t[s][:, k, tile(t)] for k in range(HT)],
                                 [w_full_a[:, k, :] for k in range(HT)])
                mm.then_inc(coefs_mm, 1)
                full_rows(0, s, banks[s][0]).then_inc(full_mm[0], 1)

            def full_scores(_, s, n, dma):
                pe.wait_ge(coefs_ready, n)
                pe.wait_ge(full_ready[0], n)
                for t in range(T):
                    tr = pe.transpose(banks[s][0][:, tile(t)], coefs[s][:, t, 1:2].to_broadcast([P, P]), ident[:, :])
                tr.then_inc(spreaded[3], 1)
                full_rows(1, s, banks[s][1]).then_inc(full_mm[1], 1)

            def turn_full(_, s, n, dma):
                pe.wait_ge(probs_ready[3], n)
                pe.wait_ge(full_ready[1], n)
                turn_tiles(banks[s][1], probs[s][:, 0, :, :]).then_inc(probs_turned[3], 1)

            def mix_full(_, s, n, dma):
                pe.wait_ge(probs_t_ready[3], n)
                for half in range(2):
                    for f in range(2):
                        mm = product(banks[s][half][:, f * NODES:(f + 1) * NODES],
                                     [h_wide[s][:, u, tile(2 * half + f)] for u in range(T)],
                                     [probs_t[s][:, 0, u, :] for u in range(T)])
                mm.then_inc(full_mixed, 1)

            def down(_, s, n, dma):
                pe.wait_ge(full_sum, n)
                for f in range(KT):
                    mm = product(banks[s][0][:, f * NODES:(f + 1) * NODES], [w_down[:, k, tile(f)] for k in range(HT)],
                                 [hid_t[s][:, k, :] for k in range(HT)])
                mm.then_inc(down_mm, 1)

            def queries_keys(_, s, n, dma):
                pe.wait_ge(norm_t_ready[3], n)
                for bank, w in ((banks[s][1], w_q), (banks[s][0], w_k)):
                    for f in range(KT):
                        mm = product(bank[:, f * NODES:(f + 1) * NODES], [w[:, k, tile(f)] for k in range(KT)],
                                     [norm_t[s][:, k, :] for k in range(KT)])
                mm.then_inc(qk_mm, 1)

            def values(_, s, n, dma):
                pe.wait_ge(q_ready, n)
                for t in range(T):
                    mm = product(banks[s][1][:, t * F:(t + 1) * F], [norm_t[s][:, k, tile(t)] for k in range(KT)],
                                 [w_v[:, k, :] for k in range(KT)])
                mm.then_inc(v_mm, 1)

            def scores(i, s, n, dma):
                pe.wait_ge(v_ready, n)
                pe.wait_ge(k_ready, n)
                if i == 1:
                    pe.wait_ge(head_top[0], n)
                for h in (2 * i, 2 * i + 1):
                    d = slice((h % 2) * HD, (h % 2 + 1) * HD)
                    for t in range(T):
                        mm = pe.matmul(banks[s][h % 2][:, t * NODES:(t + 1) * NODES], q_t[s][d, h // 2, tile(t)],
                                       k_t[s][d, h // 2, :], start=True, stop=True)
                mm.then_inc(score_mm[i], 1)

            def turn_heads(i, s, n, dma):
                pe.wait_ge(head_exps[i], n)
                pe.wait_ge([head_top[1], head_t_ready[0]][i], n)
                for h in (2 * i, 2 * i + 1):
                    tr = turn_tiles(banks[s][h % 2], probs[s][:, h, :, :])
                tr.then_inc(head_turned[i], 1)

            def mix_heads(_, s, n, dma):
                for i in range(HEADS // 2):
                    pe.wait_ge(head_t_ready[i], n)
                for t in range(T):
                    for h in range(HEADS):
                        mm = product(banks[s][0][:, t * F + h * HD:t * F + (h + 1) * HD],
                                     [probs_t[s][:, h, u, tile(t)] for u in range(T)],
                                     [vals[s][:, u, h * HD:(h + 1) * HD] for u in range(T)])
                mm.then_inc(av_mm, 1)

            def turn_heads_out(_, s, n, dma):
                pe.wait_ge(att_ready, n)
                turn_tiles(banks[s][1], att[s]).then_inc(att_turned, 1)

            def out_project(_, s, n, dma):
                pe.wait_ge(att_t_ready, n)
                for t in range(T):
                    mm = product(banks[s][0][:, t * F:(t + 1) * F], [att_t[s][:, k, tile(t)] for k in range(KT)],
                                 [w_o[:, k, :] for k in range(KT)])
                mm.then_inc(wo_mm, 1)

            run(pe, {"turn": turn, "project": project, "spread": spread, "turn_probs": turn_probs, "mix": mix,
                     "up": up, "full_coefs": full_coefs, "full_scores": full_scores, "turn_full": turn_full,
                     "mix_full": mix_full, "down": down, "queries_keys": queries_keys, "values": values,
                     "scores": scores, "turn_heads": turn_heads, "mix_heads": mix_heads,
                     "turn_heads_out": turn_heads_out, "out_project": out_project})


_INS = ["x", "adj", "L0_gnn_W", "L0_gnn_a", "L1_gnn_mlp1_w", "L1_gnn_mlp1_b", "L1_gnn_mlp2_w", "L1_gnn_mlp2_b",
        "L1_gnn_W_fc", "L1_gnn_a_fc", "L1_gnn_W_hand", "L1_gnn_a_hand", "L2_gnn_W", "L2_gnn_a", "L3_gnn_Wq",
        "L3_gnn_bq", "L3_gnn_Wk", "L3_gnn_bk", "L3_gnn_Wv", "L3_gnn_bv", "L3_gnn_Wo", "L3_gnn_bo",
        "L3_gnn_gamma", "L3_gnn_beta"]


def kernel(**inputs):
    import numpy as np
    import concourse.bacc as bacc
    from concourse import mybir
    from concourse.bass_utils import run_bass_kernel_spmd

    nc = bacc.Bacc("TRN2", target_bir_lowering=False, num_devices=1)
    arrays, args = {}, []
    for name in _INS:
        a = np.ascontiguousarray(inputs[name])
        arrays[f"in_{name}_dram"] = a
        args.append(nc.dram_tensor(f"in_{name}_dram", a.shape, mybir.dt.from_np(a.dtype), kind="ExternalInput").ap())
    args.append(nc.dram_tensor("out_0_dram", inputs["x"].shape, mybir.dt.float32, kind="ExternalOutput").ap())
    bass_graph_layers(nc, *args)
    r = run_bass_kernel_spmd(nc, [arrays], core_ids=[0])
    return r.results[0]["out_0_dram"]
```

```python
from contextlib import ExitStack

import concourse.bass as bass
from concourse import mybir

ALU = mybir.AluOpType
ACT = mybir.ActivationFunctionType
AX = mybir.AxisListType
F32 = mybir.dt.float32
I32 = mybir.dt.int32

P = 128
LANES = 4
MASKED = -1.0e30
LEAST = -3.0e38
EPS = 1e-5

PERIOD = 50000
CELL = 50
HOP = 250
PE, ACT_E, DVE, POOL = "pe", "act", "dve", "pool"


def norm_parts(i):
    return [(DVE, "stats", i, 950), (POOL, "rstd", i, 850), (DVE, "normalise", i, 650)]


def turn_parts(i):
    return [(PE, "turn", i, 270), (ACT_E, "turn", i, 480)]


def weigh_parts(i):
    return [(ACT_E, "add_f1", i, 830), (DVE, "leaky", i, 600), (ACT_E, "exps", i, 1000), (DVE, "divide", i, 750),
            (PE, "turn_probs", i, 270), (ACT_E, "turn_probs", i, 480)]


def masked_parts(g):
    return [(PE, "project", g, 1750), (ACT_E, "project", g, 480), (PE, "spread", g, 130),
            (DVE, "spread", g, 900)] + weigh_parts(g) + [(PE, "mix", g, 1750 + 270 * (g == 1))]


PARTS = (
    norm_parts(0) + turn_parts(0) + masked_parts(0) + [(DVE, "mix", 0, 600)]
    + norm_parts(1) + turn_parts(1)
    + [(PE, "up", 0, 3450), (DVE, "up", 0, 1600),
       (PE, "coefs", 0, 500), (DVE, "coefs", 0, 80), (PE, "rows", 0, 3450, ("coefs", 0)), (ACT_E, "rows", 0, 480),
       (PE, "spread", 3, 130), (DVE, "spread", 3, 450), (PE, "rows", 1, 3450, ("spread", 3)),
       (DVE, "rows", 1, 600)]
    + [(ACT_E, "add_f1", 3, 830, ("spread", 3))] + weigh_parts(3)[1:]
    + [(PE, "mix", 3, 3450), (DVE, "mix", 3, 1130), (ACT_E, "mix", 3, 2050), (DVE, "finish", 3, 1150),
       (POOL, "finish", 3, 2300), (PE, "down", 0, 3450), (ACT_E, "down", 0, 720)]
    + masked_parts(1)
    + [(DVE, "mix", 1, 600), (ACT_E, "mix", 1, 1130), (DVE, "finish", 1, 1850)]
    + norm_parts(2) + turn_parts(2) + masked_parts(2)
    + [(DVE, "mix", 2, 600), (ACT_E, "mix", 2, 520), (DVE, "finish", 2, 600), (POOL, "finish", 2, 1230)]
    + norm_parts(3) + [(POOL, "beta", 0, 1230)] + [(PE, "turn", 3, 270, ("normalise", 3)), (ACT_E, "turn", 3, 480)]
    + [(PE, "queries_keys", 0, 3450), (ACT_E, "queries", 0, 720), (DVE, "keys", 0, 800, ("queries_keys", 0)),
       (PE, "values", 0, 1750, ("queries", 0)), (DVE, "values", 0, 600),
       (PE, "scores", 0, 1750), (DVE, "scores", 0, 1500), (ACT_E, "scores", 0, 2000),
       (PE, "scores", 1, 1750, ("scores", 0, DVE)), (DVE, "scores", 1, 1500), (ACT_E, "scores", 1, 2000),
       (PE, "turn_heads", 0, 520, ("scores", 0, ACT_E), ("scores", 1, DVE)), (ACT_E, "turn_heads", 0, 900),
       (PE, "turn_heads", 1, 520, ("scores", 1, ACT_E), ("turn_heads", 0, ACT_E)), (DVE, "turn_heads", 1, 1130),
       (PE, "mix_heads", 0, 1800), (DVE, "mix_heads", 0, 750), (PE, "turn_out", 0, 270), (ACT_E, "turn_out", 0, 480),
       (PE, "out_project", 0, 1750), (DVE, "out_project", 0, 620)]
    + norm_parts(4) + [(POOL, "out", 0, 2500)]
)


HELD = {
    15: 550, 18: 850, 23: 250, 24: 1950, 25: 400, 26: 2950, 27: 2800, 28: 2800, 30: 650, 31: 2000, 32: 1700,
    33: 200, 35: 100, 36: 1750, 38: 250, 39: 350, 44: 1350, 45: 200, 50: 350, 51: 1950, 55: 950, 56: 100, 57: 150,
    61: 2150, 62: 350, 65: 150, 69: 1750, 76: 500, 77: 750, 78: 50, 81: 50, 82: 200, 83: 500, 88: 150, 90: 650,
    91: 1150, 92: 750, 99: 150, 103: 1750,
}


def timetable(engine):
    free = {e: [True] * (PERIOD // CELL) for e in (PE, ACT_E, DVE, POOL)}
    ends, last, mine = {}, 0, []
    for place, (e, step, i, ns, *after) in enumerate(PARTS):
        at = max((ends[a[0], a[1], a[2] if len(a) > 2 else None] for a in after), default=last)
        at += HELD.get(place, 0) // CELL
        start = None
        for _ in range(max(1, ns // CELL)):
            while not free[e][at % len(free[e])]:
                at += 1
            start = at if start is None else start
            free[e][at % len(free[e])] = False
            at += 1
        last = at + HOP // CELL
        ends[step, i, e] = ends[step, i, None] = last
        if e == engine:
            mine.append((start % len(free[e]), start // len(free[e]), step, i))
    assert last * CELL < (LANES - 0.05) * PERIOD, last * CELL
    return [(lag, step, i) for _, lag, step, i in sorted(mine)]


def bass_graph_layers(nc, x, adj, W0, a0, mlp1_w, mlp1_b, mlp2_w, mlp2_b, W_fc, a_fc, W_hand, a_hand,
                      W2, a2, Wq, bq, Wk, bk, Wv, bv, Wo, bo, gamma, beta, y):
    SAMPLES, NODES, F = x.shape
    H = mlp1_w.shape[1]
    T = NODES // P
    KT = F // P
    HT = H // P
    HEADS, HD = 4, F // 4
    ROUNDS = SAMPLES // LANES
    SLOPE = [0.01, 0.2, 0.2]
    FULL_SLOPE = 0.2
    SCALE = 1.0 / float(HD) ** 0.5
    assert T == 2 and KT == 2 and HT == 4 and SAMPLES % LANES == 0 and ROUNDS >= 3

    with ExitStack() as ctx:
        def sb(name, shape, dt=F32):
            return ctx.enter_context(nc.sbuf_tensor(name, shape, dt))

        def sem(name):
            return ctx.enter_context(nc.semaphore(name))

        def sems(name, n):
            return [sem(f"{name}{i}") for i in range(n)]

        w_gat = [sb(f"w_gat{g}", [P, KT, F + 2]) for g in range(3)]
        w_up = sb("w_up", [P, KT, H])
        w_full = sb("w_full", [P, HT, H])
        w_full_a = sb("w_full_a", [P, HT, 2])
        w_down = sb("w_down", [P, HT, F])
        w_q, w_k, w_v, w_o = (sb(n, [P, KT, F]) for n in ("w_q", "w_k", "w_v", "w_o"))
        b_up = sb("b_up", [P, HT])
        b_down, b_q, b_k = (sb(n, [P, KT]) for n in ("b_down", "b_q", "b_k"))
        b_v, b_o, gamma_b, beta_b = (sb(n, [P, F]) for n in ("b_v", "b_o", "gamma_b", "beta_b"))
        mask_zero = sb("mask_zero", [P, T, NODES])
        mask_neg = sb("mask_neg", [P, T, NODES])
        masks = [mask_zero, mask_neg, mask_neg]
        ident = sb("ident", [P, P])
        minus_one = sb("minus_one", [P, 1])
        minus_half = sb("minus_half", [P, T])
        eps = sb("eps", [P, T])

        def lanes(name, shape):
            return [sb(f"{name}{s}", shape) for s in range(LANES)]

        x_in = lanes("x_in", [P, T, F])
        x_cur = lanes("x_cur", [P, T, F])
        y_out = lanes("y_out", [P, T, F])
        norm = lanes("norm", [P, T, F])
        norm_t = lanes("norm_t", [P, KT, NODES])
        h_buf = lanes("h_buf", [P, T * H])
        hid_t = lanes("hid_t", [P, HT, NODES])
        low_t = lanes("low_t", [P, KT, NODES])
        probs = lanes("probs", [P, HEADS, T, NODES])
        probs_t = lanes("probs_t", [P, HEADS, T, NODES])
        stat = lanes("stat", [P, T, 6])
        mean_var = lanes("mean_var", [P, T, 2])
        var_eps = lanes("var_eps", [P, T])
        rstd = lanes("rstd", [P, T])
        top = lanes("top", [P, HEADS, T])
        neg_top = lanes("neg_top", [P, HEADS, T])
        shift = lanes("shift", [P, HEADS, T])
        sums = lanes("sums", [P, HEADS, T])
        inv = lanes("inv", [P, HEADS, T])
        coefs = lanes("coefs", [P, T, 2])
        h_wide = [b[:, :].rearrange("p (t f) -> p t f", t=T) for b in h_buf]
        h_gat = [b[:, 0:T * (F + 2)].rearrange("p (t f) -> p t f", t=T) for b in h_buf]
        vals = [b[:, 0:T * F].rearrange("p (t f) -> p t f", t=T) for b in h_buf]
        q_t = [b[:, 0:KT, :] for b in hid_t]
        k_t = [b[:, KT:2 * KT, :] for b in hid_t]
        att, att_t, out_pre = norm, low_t, norm
        pair = [ctx.enter_context(nc.psum_tensor(f"banks{s}", [P, 2, 512], F32)) for s in range(LANES)]
        banks = [[b[:, i, :] for i in range(2)] for b in pair]
        setup_adj = probs[0][:, 0, :, :].bitcast(I32)
        setup_a = probs_t[0][:, :, :, :].rearrange("p h t n -> p (h t n)")
        setup_junk = probs[1][:, 0, :, :].rearrange("p t n -> p (t n)")

        def wide(ap):
            return ap[:, :, :].rearrange("p t f -> p (t f)")

        def pair_of(buf, i):
            return buf[:, 2 * i:2 * i + 2, :, :].rearrange("p h t n -> p (h t n)")

        s_adj, s_avec, s_weights = sem("s_adj"), sem("s_avec"), sem("s_weights")
        s_ident, s_const, s_folded = sem("s_ident"), sem("s_const"), sem("s_folded")
        x_loaded, y_stored = sems("x_loaded", LANES), sems("y_stored", LANES)
        stats_made, var_ready, eps_added, rstd_ready, normed = (
            sems(n, 5) for n in ("stats_made", "var_ready", "eps_added", "rstd_ready", "normed"))
        turned, norm_t_ready = sems("turned", 4), sems("norm_t_ready", 4)
        h_mm, h_ready = sems("h_mm", 3), sems("h_ready", 3)
        spreaded, top_ready, neg_top_ready, shift_ready, scores_ready, leaky_ready, exps_ready, inv_ready, probs_ready, \
            probs_turned, probs_t_ready = (sems(n, 4) for n in (
                "spreaded", "top_ready", "neg_top_ready", "shift_ready", "scores_ready", "leaky_ready", "exps_ready", "inv_ready",
                "probs_ready", "probs_turned", "probs_t_ready"))
        mixed, x_updated = sems("mixed", 3), sems("x_updated", 3)
        low_ready, exp_low_ready, elu_ready = (
            [None] + sems(n, 2) for n in ("low_ready", "exp_low_ready", "elu_ready"))
        exp_exp_ready, sum_ready = sem("exp_exp_ready"), sem("sum_ready")
        up_mm, hid_ready, coefs_mm, coefs_ready = (
            sem(n) for n in ("up_mm", "hid_ready", "coefs_mm", "coefs_ready"))
        full_mm, full_ready = sems("full_mm", 2), sems("full_ready", 2)
        full_mixed, full_low, full_exp, full_exp_exp, full_elu, full_sum = (
            sem(n) for n in ("full_mixed", "full_low", "full_exp", "full_exp_exp", "full_elu", "full_sum"))
        down_mm, low_t_ready = sem("down_mm"), sem("low_t_ready")
        qk_mm, v_mm, q_ready, k_ready, v_ready = (sem(n) for n in ("qk_mm", "v_mm", "q_ready", "k_ready", "v_ready"))
        score_mm, head_top, head_shift, head_exps, head_turned, head_t_ready = (
            sems(n, HEADS // 2) for n in ("score_mm", "head_top", "head_shift", "head_exps", "head_turned",
                                          "head_t_ready"))
        av_mm, head_inv, att_ready, att_turned, att_t_ready = (
            sem(n) for n in ("av_mm", "head_inv", "att_ready", "att_turned", "att_t_ready"))
        wo_mm, out_pre_ready, x_beta_ready, scaled_ready, y_ready = (
            sem(n) for n in ("wo_mm", "out_pre_ready", "x_beta_ready", "scaled_ready", "y_ready"))

        x_d = x.rearrange("b (p t) f -> b p t f", t=T)
        y_d = y.rearrange("b (p t) f -> b p t f", t=T)

        def rows(w):
            return w.rearrange("(k p) f -> p k f", p=P)

        def column(b):
            return b.rearrange("(k p) -> p k", p=P)

        def everywhere(v):
            return v.rearrange("(o f) -> o f", o=1).to_broadcast([P, v.shape[0]])

        A_VECS = [(a0, 0), (a_hand, 2 * F), (a2, 4 * F)]
        WEIGHTS = [
            (w_gat[0][:, :, 0:F], rows(W0)), (w_gat[1][:, :, 0:F], rows(W_hand)), (w_gat[2][:, :, 0:F], rows(W2)),
            (w_full[:, :, :], rows(W_fc)),
            (w_up[:, :, :], rows(mlp1_w)), (w_down[:, :, :], rows(mlp2_w)),
            (w_q[:, :, :], rows(Wq)), (w_k[:, :, :], rows(Wk)), (w_v[:, :, :], rows(Wv)), (w_o[:, :, :], rows(Wo)),
            (b_up[:, :], column(mlp1_b)), (b_down[:, :], column(mlp2_b)), (b_q[:, :], column(bq)),
            (b_k[:, :], column(bk)),
            (b_v[:, :], everywhere(bv)), (b_o[:, :], everywhere(bo)), (gamma_b[:, :], everywhere(gamma)),
            (beta_b[:, :], everywhere(beta)),
        ]

        def run(eng, engine, steps):
            parts = timetable(engine)
            assert set(steps) == {step for _, step, i in parts}, engine
            for period in range(LANES):
                for lag, step, i in parts:
                    if lag <= period:
                        steps[step](i, period - lag, period - lag + 1, 16, None)
            with eng.Fori(0, ROUNDS - 1) as r:
                n_before = [eng.snap(r * LANES + (s + 1)) for s in range(LANES)]
                n_new = [eng.snap(r * LANES + (LANES + s + 1)) for s in range(LANES)]
                dma_before, dma_new = eng.snap(r * 16 + 16), eng.snap(r * 16 + 32)
                for v in n_before + n_new:
                    eng.to_reg(v)
                for period in range(LANES):
                    for lag, step, i in parts:
                        s = (period - lag) % LANES
                        if lag <= period:
                            steps[step](i, s, n_new[s], dma_new, n_before[s])
                        else:
                            steps[step](i, s, n_before[s], dma_before, None)
            for period in range(LANES):
                for lag, step, i in parts:
                    if lag > period:
                        s = (period - lag) % LANES
                        steps[step](i, s, SAMPLES - LANES + s + 1, 16 * ROUNDS, None)

        block = ctx.enter_context(nc.Block())

        @block.sync
        def _(sp):
            sp.dma_start(setup_adj, adj.rearrange("(p t) j -> p t j", t=T)).then_inc(s_adj, 16)
            sp.dma_start(setup_a[:, 0:2 * F], everywhere(a0.rearrange("f o -> (f o)"))).then_inc(s_avec, 16)
            sp.dma_start(setup_a[:, 2 * F:4 * F], everywhere(a_hand.rearrange("f o -> (f o)"))).then_inc(s_avec, 16)
            sp.dma_start(setup_a[:, 4 * F:6 * F], everywhere(a2.rearrange("f o -> (f o)"))).then_inc(s_avec, 16)
            sp.dma_start(x_in[0][:, :, :], x_d[0]).then_inc(x_loaded[0], 16)
            with nc.allow_non_contiguous_dma(reason="four bias vectors, once"):
                for dst, src in WEIGHTS:
                    sp.dma_start(dst, src).then_inc(s_weights, 16)
            sp.wait_ge(s_folded, 6 * KT)
            sp.dma_start(setup_a[:, 0:2 * H], everywhere(a_fc.rearrange("f o -> (f o)"))).then_inc(s_avec, 16)
            for s in range(LANES):
                sp.sem_inc(y_stored[s], 16)
            for s in range(1, LANES):
                sp.dma_start(x_in[s][:, :, :], x_d[s]).then_inc(x_loaded[s], 16)
            for s in range(LANES):
                sp.wait_ge(x_updated[0], s + 1)
                sp.dma_start(x_in[s][:, :, :], x_d[LANES + s]).then_inc(x_loaded[s], 16)
            with sp.Fori(0, ROUNDS - 2) as r:
                for s in range(LANES):
                    sp.wait_ge(x_updated[0], r * LANES + (LANES + s + 1))
                    sp.dma_start(x_in[s][:, :, :], x_d[r * LANES + (2 * LANES + s)]).then_inc(x_loaded[s], 16)
                    sp.wait_ge(y_ready, r * LANES + (s + 1))
                    sp.dma_start(y_d[r * LANES + s], y_out[s][:, :, :]).then_inc(y_stored[s], 16)
            for n in range((ROUNDS - 2) * LANES, SAMPLES):
                sp.wait_ge(y_ready, n + 1)
                sp.dma_start(y_d[n], y_out[n % LANES][:, :, :]).then_inc(y_stored[n % LANES], 16)
            for s in range(LANES):
                sp.wait_ge(y_stored[s], 16 * (ROUNDS + 1))

        @block.gpsimd
        def _(pool):
            pool.memset(ident[:, :], 0.0).then_inc(s_ident, 1)
            pool.memset(minus_one[:, :], -1.0).then_inc(s_const, 1)
            pool.memset(minus_half[:, :], -0.5).then_inc(s_const, 1)
            pool.memset(eps[:, :], EPS).then_inc(s_const, 1)
            pool.wait_ge(s_ident, 1)
            pool.affine_select(out=ident[:, :], in_=ident[:, :], compare_op=ALU.not_equal, fill=1.0, base=0,
                               pattern=[[-1, P]], channel_multiplier=1).then_inc(s_ident, 1)
            pool.wait_ge(s_const, 3)
            pool.wait_ge(s_weights, 16 * len(WEIGHTS))

            def rstd_(l, s, n, dma, before):
                pool.wait_ge(var_ready[l], n)
                pool.tensor_tensor(var_eps[s][:, :], mean_var[s][:, :, 1], eps[:, :], ALU.add)\
                    .then_inc(eps_added[l], 1)
                pool.wait_ge(eps_added[l], n)
                pool.tensor_tensor(rstd[s][:, :], var_eps[s][:, :], minus_half[:, :], ALU.pow)\
                    .then_inc(rstd_ready[l], 1)

            def finish(g, s, n, dma, before):
                if g == 3:
                    pool.wait_ge(full_elu, n)
                    pool.tensor_tensor(wide(hid_t[s]), wide(hid_t[s]), pair_of(probs_t[s], 1), ALU.add)\
                        .then_inc(full_sum, 1)
                else:
                    pool.wait_ge(elu_ready[2], n)
                    pool.tensor_tensor(x_cur[s][:, :, :], x_cur[s][:, :, :], probs[s][:, 1, :, :], ALU.add)\
                        .then_inc(x_updated[2], 1)

            def beta_(_, s, n, dma, before):
                pool.wait_ge(normed[3], n)
                pool.tensor_tensor(x_cur[s][:, :, :], x_cur[s][:, :, :],
                                   beta_b[:, :].unsqueeze(1).to_broadcast([P, T, F]), ALU.add)\
                    .then_inc(x_beta_ready, 1)

            def out(_, s, n, dma, before):
                pool.wait_ge(normed[4], n)
                pool.tensor_tensor(norm[s][:, :, :], norm[s][:, :, :],
                                   gamma_b[:, :].unsqueeze(1).to_broadcast([P, T, F]), ALU.mult)\
                    .then_inc(scaled_ready, 1)
                pool.wait_ge(scaled_ready, n)
                pool.wait_ge(x_beta_ready, n)
                pool.wait_ge(y_stored[s], dma)
                pool.tensor_tensor(y_out[s][:, :, :], norm[s][:, :, :], x_cur[s][:, :, :], ALU.add)\
                    .then_inc(y_ready, 1)

            run(pool, POOL, {"rstd": rstd_, "finish": finish, "beta": beta_, "out": out})

        @block.scalar
        def _(act):
            act.preload_act_table(ACT.Exp)
            act.wait_ge(s_const, 3)
            act.wait_ge(s_weights, 16 * len(WEIGHTS))
            act.wait_ge(s_folded, 6 * KT + 2 * HT)

            def turn(l, s, n, dma, before):
                act.wait_ge(turned[l], n)
                act.activation(wide(norm_t[s]), banks[s][0][:, :], ACT.Relu).then_inc(norm_t_ready[l], 1)

            def project(g, s, n, dma, before):
                act.wait_ge(h_mm[g], n)
                act.activation(h_gat[s], pair[s][:, :, 0:F + 2], ACT.Copy).then_inc(h_ready[g], 1)

            def biased(g, s, n, src, column_of):
                for t in range(T):
                    add = act.activation(probs[s][:, 0, t, :], src(t), ACT.Identity, bias=column_of(t))
                add.then_inc(scores_ready[g], 1)

            def add_f1(g, s, n, dma, before):
                act.wait_ge(top_ready[g], n)
                if g == 3:
                    biased(3, s, n, lambda t: banks[s][0][:, 0:NODES], lambda t: coefs[s][:, t, 0:1])
                else:
                    biased(g, s, n, lambda t: probs[s][:, 0, t, :], lambda t: h_gat[s][:, t, F:F + 1])

            def exps(g, s, n, dma, before):
                act.wait_ge(leaky_ready[g], n)
                act.wait_ge(shift_ready[g], n)
                for t in range(T):
                    ex = act.activation(probs[s][:, 0, t, :], probs[s][:, 0, t, :], ACT.Exp,
                                        bias=shift[s][:, 0, t:t + 1], accum_out=sums[s][:, 0, t:t + 1])
                ex.then_inc(exps_ready[g], 1)

            def turn_probs(g, s, n, dma, before):
                act.wait_ge(probs_turned[g], n)
                act.activation(wide(probs_t[s][:, 0, :, :]), banks[s][1 if g == 3 else 0][:, :], ACT.Copy)\
                    .then_inc(probs_t_ready[g], 1)

            def mix(g, s, n, dma, before):
                if g == 3:
                    low = pair_of(probs[s], 1)
                    act.wait_ge(full_low, n)
                    act.activation(low, low, ACT.Exp).then_inc(full_exp, 1)
                    act.wait_ge(full_exp, n)
                    act.activation(low, low, ACT.Exp, bias=minus_one[:, 0:1]).then_inc(full_exp_exp, 1)
                    return
                act.wait_ge(low_ready[g], n)
                act.activation(probs[s][:, 2, :, :], probs[s][:, 2, :, :], ACT.Exp).then_inc(exp_low_ready[g], 1)
                if g == 1:
                    act.wait_ge(exp_low_ready[1], n)
                    act.activation(probs[s][:, 2, :, :], probs[s][:, 2, :, :], ACT.Exp, bias=minus_one[:, 0:1])\
                        .then_inc(exp_exp_ready, 1)

            def rows_(_, s, n, dma, before):
                act.wait_ge(full_mm[0], n)
                act.activation(h_wide[s][:, 0, :], banks[s][0][:, :], ACT.Copy).then_inc(full_ready[0], 1)

            def down(_, s, n, dma, before):
                act.wait_ge(down_mm, n)
                for f in range(KT):
                    relu = act.activation(low_t[s][:, f, :], banks[s][0][:, f * NODES:(f + 1) * NODES], ACT.Relu,
                                          bias=b_down[:, f:f + 1])
                relu.then_inc(low_t_ready, 1)

            def queries(_, s, n, dma, before):
                act.wait_ge(qk_mm, n)
                for f in range(KT):
                    q = act.activation(q_t[s][:, f, :], banks[s][1][:, f * NODES:(f + 1) * NODES], ACT.Identity,
                                       bias=b_q[:, f:f + 1])
                q.then_inc(q_ready, 1)

            def scores(i, s, n, dma, before):
                act.wait_ge(head_shift[i], n)
                for h in (2 * i, 2 * i + 1):
                    for t in range(T):
                        ex = act.activation(probs[s][:, h, t, :], probs[s][:, h, t, :], ACT.Exp,
                                            bias=shift[s][:, h, t:t + 1], scale=SCALE,
                                            accum_out=sums[s][:, h, t:t + 1])
                ex.then_inc(head_exps[i], 1)

            def turn_heads(i, s, n, dma, before):
                act.wait_ge(head_turned[0], n)
                act.activation(pair_of(probs_t[s], 0), wide(pair[s]), ACT.Copy).then_inc(head_t_ready[0], 1)

            def turn_out(_, s, n, dma, before):
                act.wait_ge(att_turned, n)
                act.activation(wide(att_t[s]), banks[s][1][:, :], ACT.Copy).then_inc(att_t_ready, 1)

            run(act, ACT_E, {"turn": turn, "project": project, "add_f1": add_f1, "exps": exps, "turn_probs": turn_probs,
                             "mix": mix, "rows": rows_, "down": down, "queries": queries, "scores": scores,
                             "turn_heads": turn_heads, "turn_out": turn_out})

        @block.vector
        def _(dve):
            dve.wait_ge(s_weights, 16 * len(WEIGHTS))
            dve.wait_ge(s_adj, 16)
            by_tile = setup_adj.rearrange("p t (q u) -> p t u q", u=T)
            for t in range(T):
                for mask, test in ((mask_zero, ALU.is_equal), (mask_neg, ALU.is_le)):
                    dve.tensor_scalar(mask[:, t, :].rearrange("p (u q) -> p u q", u=T), by_tile[:, t], 0.0, MASKED,
                                      test, ALU.mult).then_inc(s_const, 1)
            dve.wait_ge(s_avec, 48)
            folds = 0
            for g in range(3):
                for k in range(KT):
                    for half in range(2):
                        a = setup_a[:, (2 * g + half) * F:(2 * g + half + 1) * F]
                        if folds:
                            dve.wait_ge(s_folded, folds)
                        dve.tensor_tensor_reduce(setup_junk[:, 0:F], w_gat[g][:, k, 0:F], a, 1.0, 0.0, ALU.mult,
                                                 ALU.add, w_gat[g][:, k, F + half:F + half + 1]).then_inc(s_folded, 1)
                        folds += 1
            dve.wait_ge(s_avec, 64)
            for k in range(HT):
                for half in range(2):
                    dve.wait_ge(s_folded, folds)
                    dve.tensor_tensor_reduce(setup_junk[:, 0:H], w_full[:, k, :], setup_a[:, half * H:(half + 1) * H],
                                             1.0, 0.0, ALU.mult, ALU.add, w_full_a[:, k, half:half + 1])\
                        .then_inc(s_folded, 1)
                    folds += 1
            assert folds == 6 * KT + 2 * HT
            dve.wait_ge(s_folded, folds)
            dve.wait_ge(s_const, 3 + 2 * T)

            def normalise(l, s, n, dma, before):
                dve.wait_ge(rstd_ready[l], n)
                src = x_in[s] if l == 0 else norm[s] if l == 4 else x_cur[s]
                for t in range(T):
                    nm = dve.tensor_scalar(norm[s][:, t, :], src[:, t, :], mean_var[s][:, t, 0:1],
                                           rstd[s][:, t:t + 1], ALU.subtract, ALU.mult)
                nm.then_inc(normed[l], 1)

            def stats(l, s, n, dma, before):
                if l == 0:
                    if before is not None:
                        dve.wait_ge(y_ready, before)
                    dve.wait_ge(x_loaded[s], dma)
                elif l == 4:
                    dve.wait_ge(out_pre_ready, n)
                else:
                    dve.wait_ge(x_updated[l - 1], n)
                src = x_in[s] if l == 0 else out_pre[s] if l == 4 else x_cur[s]
                for t in range(T):
                    st = dve.bn_stats(stat[s][:, t, :], src[:, t, :])
                st.then_inc(stats_made[l], 1)
                dve.wait_ge(s_const, 3)
                dve.wait_ge(stats_made[l], n)
                for t in range(T):
                    ag = dve.bn_aggr(mean_var[s][:, t, :], stat[s][:, t, :])
                ag.then_inc(var_ready[l], 1)

            def spread(g, s, n, dma, before):
                if g == 3:
                    dve.wait_ge(spreaded[3], n)
                    dve.tensor_reduce(top[s][:, 0, 0:1], banks[s][0][:, 0:NODES], AX.X, ALU.max)\
                        .then_inc(top_ready[3], 1)
                    dve.wait_ge(top_ready[3], n)
                    dve.tensor_scalar(neg_top[s][:, 0, :], coefs[s][:, :, 0], -1.0, top[s][:, 0, 0:1], ALU.mult,
                                      ALU.subtract).then_inc(neg_top_ready[3], 1)
                    dve.wait_ge(neg_top_ready[3], n)
                    dve.scalar_tensor_tensor(out=shift[s][:, 0, :], in0=neg_top[s][:, 0, :], scalar=FULL_SLOPE,
                                             in1=neg_top[s][:, 0, :], op0=ALU.mult, op1=ALU.min)\
                        .then_inc(shift_ready[3], 1)
                    return
                dve.wait_ge(s_const, 3)
                dve.wait_ge(spreaded[g], n)
                for t in range(T):
                    tt = dve.tensor_tensor_reduce(probs[s][:, 0, t, :], banks[s][1][:, 0:NODES], masks[g][:, t, :],
                                                  1.0, LEAST, ALU.add, ALU.max, top[s][:, 0, t:t + 1])
                tt.then_inc(top_ready[g], 1)
                dve.wait_ge(top_ready[g], n)
                dve.scalar_tensor_tensor(out=neg_top[s][:, 0, :], in0=top[s][:, 0, :], scalar=-1.0,
                                         in1=h_gat[s][:, :, F], op0=ALU.mult, op1=ALU.subtract)\
                    .then_inc(neg_top_ready[g], 1)
                dve.wait_ge(neg_top_ready[g], n)
                dve.scalar_tensor_tensor(out=shift[s][:, 0, :], in0=neg_top[s][:, 0, :], scalar=SLOPE[g],
                                         in1=neg_top[s][:, 0, :], op0=ALU.mult, op1=ALU.min)\
                    .then_inc(shift_ready[g], 1)

            def leaky(g, s, n, dma, before):
                slope = (SLOPE + [FULL_SLOPE])[g]
                row = probs[s][:, 0, :, :].rearrange("p t n -> p (t n)")
                dve.wait_ge(scores_ready[g], n)
                dve.scalar_tensor_tensor(out=row, in0=row, scalar=slope, in1=row, op0=ALU.mult, op1=ALU.max)\
                    .then_inc(leaky_ready[g], 1)

            def divide(g, s, n, dma, before):
                dve.wait_ge(exps_ready[g], n)
                dve.reciprocal(inv[s][:, 0, :], sums[s][:, 0, :]).then_inc(inv_ready[g], 1)
                dve.wait_ge(inv_ready[g], n)
                for t in range(T):
                    pr = dve.tensor_scalar(probs[s][:, 0, t, :], probs[s][:, 0, t, :], inv[s][:, 0, t:t + 1], None,
                                           ALU.mult)
                pr.then_inc(probs_ready[g], 1)

            def mix(g, s, n, dma, before):
                if g == 3:
                    dve.wait_ge(full_mixed, n)
                    dve.tensor_scalar(pair_of(probs[s], 1), wide(pair[s]), 0.0, None, ALU.min).then_inc(full_low, 1)
                    return
                dve.wait_ge(mixed[g], n)
                if g == 0:
                    dve.scalar_tensor_tensor(out=wide(x_cur[s]), in0=banks[s][1][:, :], scalar=0.0,
                                             in1=wide(x_in[s]), op0=ALU.max, op1=ALU.add).then_inc(x_updated[0], 1)
                else:
                    dve.tensor_scalar(wide(probs[s][:, 2, :, :]), banks[s][1][:, :], 0.0, None, ALU.min)\
                        .then_inc(low_ready[g], 1)

            def finish(g, s, n, dma, before):
                if g == 3:
                    dve.wait_ge(full_exp_exp, n)
                    dve.scalar_tensor_tensor(out=pair_of(probs_t[s], 1), in0=pair_of(probs[s], 1), scalar=-1.0,
                                             in1=wide(pair[s]), op0=ALU.add, op1=ALU.max).then_inc(full_elu, 1)
                    return
                dve.wait_ge(exp_exp_ready if g == 1 else exp_low_ready[2], n)
                dve.scalar_tensor_tensor(out=wide(probs[s][:, 1, :, :]), in0=wide(probs[s][:, 2, :, :]), scalar=-1.0,
                                         in1=banks[s][1][:, :], op0=ALU.add, op1=ALU.max).then_inc(elu_ready[g], 1)
                if g == 1:
                    dve.wait_ge(elu_ready[1], n)
                    dve.tensor_tensor(wide(probs[s][:, 1, :, :]), banks[s][0][:, :], wide(probs[s][:, 1, :, :]),
                                      ALU.add).then_inc(sum_ready, 1)
                    dve.wait_ge(sum_ready, n)
                    dve.scalar_tensor_tensor(out=wide(x_cur[s]), in0=wide(probs[s][:, 1, :, :]), scalar=0.0,
                                             in1=wide(x_cur[s]), op0=ALU.max, op1=ALU.add).then_inc(x_updated[1], 1)

            def up(_, s, n, dma, before):
                dve.wait_ge(up_mm, n)
                for f in range(HT):
                    relu = dve.tensor_scalar(hid_t[s][:, f, :], banks[s][f // 2][:, (f % 2) * NODES:][:, 0:NODES],
                                             b_up[:, f:f + 1], 0.0, ALU.add, ALU.max)
                relu.then_inc(hid_ready, 1)

            def coefs_(_, s, n, dma, before):
                dve.wait_ge(coefs_mm, n)
                dve.tensor_copy(wide(coefs[s]), banks[s][1][:, 0:2 * T]).then_inc(coefs_ready, 1)

            def rows_(_, s, n, dma, before):
                dve.wait_ge(full_mm[1], n)
                dve.tensor_copy(h_wide[s][:, 1, :], banks[s][1][:, :]).then_inc(full_ready[1], 1)

            def keys(_, s, n, dma, before):
                dve.wait_ge(qk_mm, n)
                for f in range(KT):
                    k = dve.tensor_scalar(k_t[s][:, f, :], banks[s][0][:, f * NODES:(f + 1) * NODES], b_k[:, f:f + 1],
                                          None, ALU.add)
                k.then_inc(k_ready, 1)

            def values(_, s, n, dma, before):
                dve.wait_ge(v_mm, n)
                dve.tensor_tensor(vals[s], banks[s][1][:, :].rearrange("p (t f) -> p t f", t=T),
                                  b_v[:, :].unsqueeze(1).to_broadcast([P, T, F]), ALU.add).then_inc(v_ready, 1)

            def scores(i, s, n, dma, before):
                dve.wait_ge(s_const, 3)
                dve.wait_ge(score_mm[i], n)
                for h in (2 * i, 2 * i + 1):
                    for t in range(T):
                        tt = dve.tensor_tensor_reduce(probs[s][:, h, t, :],
                                                      banks[s][h % 2][:, t * NODES:(t + 1) * NODES],
                                                      mask_zero[:, t, :], 1.0, LEAST, ALU.add, ALU.max,
                                                      top[s][:, h, t:t + 1])
                tt.then_inc(head_top[i], 1)
                dve.wait_ge(head_top[i], n)
                dve.tensor_scalar(shift[s][:, 2 * i:2 * i + 2, :], top[s][:, 2 * i:2 * i + 2, :], -SCALE, None,
                                  ALU.mult).then_inc(head_shift[i], 1)

            def turn_heads(i, s, n, dma, before):
                dve.wait_ge(head_turned[1], n)
                dve.tensor_copy(pair_of(probs_t[s], 1), wide(pair[s])).then_inc(head_t_ready[1], 1)

            def mix_heads(_, s, n, dma, before):
                dve.wait_ge(head_exps[1], n)
                dve.reciprocal(inv[s][:, :, :], sums[s][:, :, :]).then_inc(head_inv, 1)
                dve.wait_ge(head_inv, n)
                dve.wait_ge(av_mm, n)
                dve.tensor_tensor(att[s][:, :, :].rearrange("p t (h d) -> p t h d", h=HEADS),
                                  banks[s][0][:, :].rearrange("p (t h d) -> p t h d", t=T, h=HEADS),
                                  inv[s][:, :, :].rearrange("p h t -> p t h").unsqueeze(3)
                                  .to_broadcast([P, T, HEADS, HD]), ALU.mult).then_inc(att_ready, 1)

            def out_project(_, s, n, dma, before):
                dve.wait_ge(wo_mm, n)
                dve.tensor_tensor(out_pre[s][:, :, :], banks[s][0][:, :].rearrange("p (t f) -> p t f", t=T),
                                  b_o[:, :].unsqueeze(1).to_broadcast([P, T, F]), ALU.add)\
                    .then_inc(out_pre_ready, 1)

            run(dve, DVE, {"stats": stats, "normalise": normalise, "spread": spread, "leaky": leaky, "divide": divide,
                           "mix": mix, "finish": finish, "up": up, "coefs": coefs_, "rows": rows_, "keys": keys,
                           "values": values, "scores": scores, "turn_heads": turn_heads, "mix_heads": mix_heads,
                           "out_project": out_project})

        @block.tensor
        def _(pe):
            pe.wait_ge(s_ident, 2)
            pe.wait_ge(s_weights, 16 * len(WEIGHTS))
            pe.wait_ge(s_folded, 6 * KT + 2 * HT)

            def product(out, lhs, rhs):
                for k, (a, b) in enumerate(zip(lhs, rhs)):
                    mm = pe.matmul(out, a, b, start=(k == 0), stop=(k == len(lhs) - 1))
                return mm

            def turn_tiles(bank, src):
                for a in range(2):
                    for b in range(2):
                        tr = pe.transpose(bank[:, b * 2 * P + a * P:b * 2 * P + (a + 1) * P],
                                          src[:, a, b * P:(b + 1) * P], ident[:, :])
                return tr

            def tile(t):
                return slice(t * P, (t + 1) * P)

            def turn(l, s, n, dma, before):
                pe.wait_ge(normed[l], n)
                turn_tiles(banks[s][0], norm[s]).then_inc(turned[l], 1)

            def project(g, s, n, dma, before):
                src = low_t[s] if g == 1 else norm_t[s]
                pe.wait_ge(low_t_ready if g == 1 else norm_t_ready[[0, None, 2][g]], n)
                for t in range(T):
                    mm = product(banks[s][t][:, 0:F + 2], [src[:, k, tile(t)] for k in range(KT)],
                                 [w_gat[g][:, k, :] for k in range(KT)])
                mm.then_inc(h_mm[g], 1)

            def spread(g, s, n, dma, before):
                if g == 3:
                    pe.wait_ge(coefs_ready, n)
                    pe.wait_ge(full_ready[0], n)
                    for t in range(T):
                        tr = pe.transpose(banks[s][0][:, tile(t)], coefs[s][:, t, 1:2].to_broadcast([P, P]),
                                          ident[:, :])
                    tr.then_inc(spreaded[3], 1)
                    return
                pe.wait_ge(h_ready[g], n)
                for t in range(T):
                    tr = pe.transpose(banks[s][1][:, tile(t)], h_gat[s][:, t, F + 1:F + 2].to_broadcast([P, P]),
                                      ident[:, :])
                tr.then_inc(spreaded[g], 1)

            def turn_probs(g, s, n, dma, before):
                pe.wait_ge(probs_ready[g], n)
                if g == 3:
                    pe.wait_ge(full_ready[1], n)
                turn_tiles(banks[s][1 if g == 3 else 0], probs[s][:, 0, :, :]).then_inc(probs_turned[g], 1)

            def mix(g, s, n, dma, before):
                pe.wait_ge(probs_t_ready[g], n)
                if g == 3:
                    for half in range(2):
                        for f in range(2):
                            mm = product(banks[s][half][:, f * NODES:(f + 1) * NODES],
                                         [h_wide[s][:, u, tile(2 * half + f)] for u in range(T)],
                                         [probs_t[s][:, 0, u, :] for u in range(T)])
                    mm.then_inc(full_mixed, 1)
                    return
                for t in range(T):
                    mm = product(banks[s][1][:, t * F:(t + 1) * F],
                                 [probs_t[s][:, 0, u, tile(t)] for u in range(T)],
                                 [h_gat[s][:, u, 0:F] for u in range(T)])
                if g == 1:
                    mm = turn_tiles(banks[s][0], low_t[s])
                mm.then_inc(mixed[g], 1)

            def up(_, s, n, dma, before):
                pe.wait_ge(norm_t_ready[1], n)
                for half in range(2):
                    for f in range(2):
                        mm = product(banks[s][half][:, f * NODES:(f + 1) * NODES],
                                     [w_up[:, k, tile(2 * half + f)] for k in range(KT)],
                                     [norm_t[s][:, k, :] for k in range(KT)])
                mm.then_inc(up_mm, 1)

            def coefs_(_, s, n, dma, before):
                pe.wait_ge(hid_ready, n)
                for t in range(T):
                    mm = product(banks[s][1][:, 2 * t:2 * t + 2], [hid_t[s][:, k, tile(t)] for k in range(HT)],
                                 [w_full_a[:, k, :] for k in range(HT)])
                mm.then_inc(coefs_mm, 1)

            def rows_(t, s, n, dma, before):
                if t == 1:
                    pe.wait_ge(coefs_ready, n)
                product(banks[s][t][:, :], [hid_t[s][:, k, tile(t)] for k in range(HT)],
                        [w_full[:, k, :] for k in range(HT)]).then_inc(full_mm[t], 1)

            def down(_, s, n, dma, before):
                pe.wait_ge(full_sum, n)
                for f in range(KT):
                    mm = product(banks[s][0][:, f * NODES:(f + 1) * NODES], [w_down[:, k, tile(f)] for k in range(HT)],
                                 [hid_t[s][:, k, :] for k in range(HT)])
                mm.then_inc(down_mm, 1)

            def queries_keys(_, s, n, dma, before):
                pe.wait_ge(norm_t_ready[3], n)
                for bank, w in ((banks[s][1], w_q), (banks[s][0], w_k)):
                    for f in range(KT):
                        mm = product(bank[:, f * NODES:(f + 1) * NODES], [w[:, k, tile(f)] for k in range(KT)],
                                     [norm_t[s][:, k, :] for k in range(KT)])
                mm.then_inc(qk_mm, 1)

            def values(_, s, n, dma, before):
                pe.wait_ge(q_ready, n)
                for t in range(T):
                    mm = product(banks[s][1][:, t * F:(t + 1) * F], [norm_t[s][:, k, tile(t)] for k in range(KT)],
                                 [w_v[:, k, :] for k in range(KT)])
                mm.then_inc(v_mm, 1)

            def scores(i, s, n, dma, before):
                pe.wait_ge(v_ready, n)
                pe.wait_ge(k_ready, n)
                if i == 1:
                    pe.wait_ge(head_top[0], n)
                for h in (2 * i, 2 * i + 1):
                    d = slice((h % 2) * HD, (h % 2 + 1) * HD)
                    for t in range(T):
                        mm = pe.matmul(banks[s][h % 2][:, t * NODES:(t + 1) * NODES], q_t[s][d, h // 2, tile(t)],
                                       k_t[s][d, h // 2, :], start=True, stop=True)
                mm.then_inc(score_mm[i], 1)

            def turn_heads(i, s, n, dma, before):
                pe.wait_ge(head_exps[i], n)
                pe.wait_ge([head_top[1], head_t_ready[0]][i], n)
                for h in (2 * i, 2 * i + 1):
                    tr = turn_tiles(banks[s][h % 2], probs[s][:, h, :, :])
                tr.then_inc(head_turned[i], 1)

            def mix_heads(_, s, n, dma, before):
                for i in range(HEADS // 2):
                    pe.wait_ge(head_t_ready[i], n)
                for t in range(T):
                    for h in range(HEADS):
                        mm = product(banks[s][0][:, t * F + h * HD:t * F + (h + 1) * HD],
                                     [probs_t[s][:, h, u, tile(t)] for u in range(T)],
                                     [vals[s][:, u, h * HD:(h + 1) * HD] for u in range(T)])
                mm.then_inc(av_mm, 1)

            def turn_out(_, s, n, dma, before):
                pe.wait_ge(att_ready, n)
                turn_tiles(banks[s][1], att[s]).then_inc(att_turned, 1)

            def out_project(_, s, n, dma, before):
                pe.wait_ge(att_t_ready, n)
                for t in range(T):
                    mm = product(banks[s][0][:, t * F:(t + 1) * F], [att_t[s][:, k, tile(t)] for k in range(KT)],
                                 [w_o[:, k, :] for k in range(KT)])
                mm.then_inc(wo_mm, 1)

            run(pe, PE, {"turn": turn, "project": project, "spread": spread, "turn_probs": turn_probs, "mix": mix,
                         "up": up, "coefs": coefs_, "rows": rows_, "down": down, "queries_keys": queries_keys,
                         "values": values, "scores": scores, "turn_heads": turn_heads, "mix_heads": mix_heads,
                         "turn_out": turn_out, "out_project": out_project})


_INS = ["x", "adj", "L0_gnn_W", "L0_gnn_a", "L1_gnn_mlp1_w", "L1_gnn_mlp1_b", "L1_gnn_mlp2_w", "L1_gnn_mlp2_b",
        "L1_gnn_W_fc", "L1_gnn_a_fc", "L1_gnn_W_hand", "L1_gnn_a_hand", "L2_gnn_W", "L2_gnn_a", "L3_gnn_Wq",
        "L3_gnn_bq", "L3_gnn_Wk", "L3_gnn_bk", "L3_gnn_Wv", "L3_gnn_bv", "L3_gnn_Wo", "L3_gnn_bo",
        "L3_gnn_gamma", "L3_gnn_beta"]


def kernel(**inputs):
    import numpy as np
    import concourse.bacc as bacc
    from concourse import mybir
    from concourse.bass_utils import run_bass_kernel_spmd

    nc = bacc.Bacc("TRN2", target_bir_lowering=False, num_devices=1)
    arrays, args = {}, []
    for name in _INS:
        a = np.ascontiguousarray(inputs[name])
        arrays[f"in_{name}_dram"] = a
        args.append(nc.dram_tensor(f"in_{name}_dram", a.shape, mybir.dt.from_np(a.dtype), kind="ExternalInput").ap())
    args.append(nc.dram_tensor("out_0_dram", inputs["x"].shape, mybir.dt.float32, kind="ExternalOutput").ap())
    bass_graph_layers(nc, *args)
    r = run_bass_kernel_spmd(nc, [arrays], core_ids=[0])
    return r.results[0]["out_0_dram"]
```

```python
from contextlib import ExitStack

import concourse.bass as bass
from concourse import mybir

ALU = mybir.AluOpType
ACT = mybir.ActivationFunctionType
AX = mybir.AxisListType
F32 = mybir.dt.float32
F32R = mybir.dt.float32r
I32 = mybir.dt.int32

P = 128
LANES = 4
MASKED = -1.0e30
LEAST = -3.0e38
EPS = 1e-5

PERIOD = 44148
PE, ACT_E, DVE, POOL = "pe", "act", "dve", "pool"


def norm_parts(i):
    return [(DVE, "stats", i, 1050), (POOL, "rstd", i, 900), (DVE, "normalise", i, 650)]


def turn_parts(i):
    return [(PE, "turn", i, 450), (ACT_E, "turn", i, 500)] + [(DVE, "norm_low", i, 600)] * (i in (1, 3))


def weigh_parts(i):
    return [(ACT_E, "add_f1", i, 800), (DVE, "leaky", i, 600), (ACT_E, "exps", i, 1000), (DVE, "divide", i, 750),
            (PE, "turn_probs", i, 450), (ACT_E, "turn_probs", i, 500)] + [(DVE, "probs_low", i, 600)] * (i == 3)


def masked_parts(g):
    return [(PE, "project", g, 1750), (ACT_E, "project", g, 500), (PE, "spread", g, 250),
            (DVE, "spread", g, 1050)] + weigh_parts(g) + [(PE, "mix", g, 1750 + 450 * (g == 1))]


PARTS = (
    norm_parts(0) + turn_parts(0) + masked_parts(0) + [(DVE, "mix", 0, 600)]
    + norm_parts(1) + turn_parts(1)
    + [(PE, "up", 0, 2600), (ACT_E, "up", 0, 1450), (ACT_E, "hid_high", 0, 950), (POOL, "hid_low", 0, 1225),
       (DVE, "hid_low", 0, 600, ("hid_high", 0, ACT_E)),
       (PE, "rows", 0, 2650, ("hid_low", 0, POOL), ("hid_low", 0, DVE)), (ACT_E, "rows", 0, 500),
       (DVE, "rows_low", 0, 700),
       (PE, "rows", 1, 2650), (ACT_E, "rows", 1, 500), (DVE, "rows_low", 1, 700),
       (PE, "spread", 3, 250), (DVE, "spread", 3, 800)]
    + weigh_parts(3)
    + [(PE, "mix", 3, 2600), (ACT_E, "mix", 3, 3250), (DVE, "finish", 3, 1150),
       (POOL, "finish", 3, 2300), (ACT_E, "hid_high", 1, 950), (POOL, "hid_low", 1, 1225),
       (DVE, "hid_low", 1, 600, ("hid_high", 1, ACT_E)),
       (PE, "down", 0, 2600, ("hid_low", 1, POOL), ("hid_low", 1, DVE)), (ACT_E, "down", 0, 700)]
    + masked_parts(1)
    + [(ACT_E, "mix", 1, 1900), (DVE, "finish", 1, 2050)]
    + norm_parts(2) + turn_parts(2) + masked_parts(2)
    + [(ACT_E, "mix", 2, 1150), (DVE, "finish", 2, 600), (POOL, "finish", 2, 1250)]
    + norm_parts(3) + [(POOL, "beta", 0, 1250), (PE, "turn", 3, 450, ("normalise", 3)), (ACT_E, "turn", 3, 500),
       (DVE, "norm_low", 3, 600)]
    + [(PE, "qk", 0, 1300), (PE, "qk", 1, 1300), (ACT_E, "qk", 0, 725, ("qk", 0, PE)), (DVE, "qk_low", 0, 800),
       (ACT_E, "qk", 1, 725, ("qk", 1, PE), ("qk", 0, ACT_E)), (DVE, "qk_low", 1, 800),
       (PE, "values", 0, 1300, ("qk_low", 0, DVE), ("qk", 1, PE)),
       (DVE, "values", 0, 600, ("values", 0, PE), ("qk_low", 1, DVE)),
       (PE, "scores", 0, 1300), (DVE, "scores", 0, 1550), (ACT_E, "scores", 0, 2000),
       (PE, "scores", 1, 1300, ("scores", 0, DVE)), (DVE, "scores", 1, 1550), (ACT_E, "scores", 1, 2000),
       (PE, "turn_heads", 0, 850, ("scores", 0, ACT_E), ("scores", 1, DVE)), (ACT_E, "turn_heads", 0, 900),
       (PE, "turn_heads", 1, 850, ("scores", 1, ACT_E), ("turn_heads", 0, ACT_E)), (ACT_E, "turn_heads", 1, 900),
       (PE, "mix_heads", 0, 3400), (DVE, "mix_heads", 0, 750), (PE, "turn_out", 0, 450), (ACT_E, "turn_out", 0, 500),
       (PE, "out_project", 0, 1750), (DVE, "out_project", 0, 600)]
    + norm_parts(4) + [(POOL, "out", 0, 2600)]
)


STARTS = [
    13923, 15204, 16809, 23896, 25129, 27659, 27881, 28413, 33029, 33029, 34851, 37461, 39901, 40798, 41914, 43162,
    45491, 46268, 46889, 47246, 47498, 47976, 49474, 50219, 53129, 53171, 57362, 56357, 58162, 59617, 62105, 67750,
    68128, 70117, 70724, 70988, 71779, 72437, 77771, 80969, 81356, 81774, 84266, 85738, 89101, 92717, 94732, 95256,
    97355, 98482, 99652, 100212, 103828, 103858, 108711, 109994, 110702, 113857, 115614, 115615, 117926, 120294,
    124340, 126932, 130189, 130257, 132543, 133323, 133387, 134245, 134426, 137019, 137901, 137955, 138622, 139486,
    139672, 141259, 141386, 144346, 144820, 145426, 148385, 149395, 149887, 150594, 150763, 212771, 153054, 153392,
    157190, 158881, 160717, 159915, 160182, 163860, 166216, 162557, 166259, 171493, 173275, 173332, 174152, 177030,
    178916, 177725, 180293, 180734, 181640, 182874, 188783, 190084, 190392, 194771, 197783, 201492, 208171, 215746,
    216819,
]
assert len(STARTS) == len(PARTS)


def timetable(engine):
    mine = [(start % PERIOD, start // PERIOD, step, i)
            for start, (e, step, i, *_) in zip(STARTS, PARTS) if e == engine]
    return [(lag, step, i) for _, lag, step, i in sorted(mine)]


def bass_graph_layers(nc, x, adj, W0, a0, mlp1_w, mlp1_b, mlp2_w, mlp2_b, W_fc, a_fc, W_hand, a_hand,
                      W2, a2, Wq, bq, Wk, bk, Wv, bv, Wo, bo, gamma, beta, y):
    SAMPLES, NODES, F = x.shape
    H = mlp1_w.shape[1]
    T = NODES // P
    KT = F // P
    HT = H // P
    HEADS, HD = 4, F // 4
    ROUNDS = SAMPLES // LANES
    SLOPE = [0.01, 0.2, 0.2]
    FULL_SLOPE = 0.2
    SCALE = 1.0 / float(HD) ** 0.5
    assert T == 2 and KT == 2 and HT == 4 and SAMPLES % LANES == 0 and ROUNDS >= 3

    with ExitStack() as ctx:
        def sb(name, shape, dt=F32):
            return ctx.enter_context(nc.sbuf_tensor(name, shape, dt))

        def sem(name):
            return ctx.enter_context(nc.semaphore(name))

        def sems(name, n):
            return [sem(f"{name}{i}") for i in range(n)]

        w_gat = [sb(f"w_gat{g}", [P, KT, F + 2]) for g in range(3)]
        def parts_of(name, shape):
            return sb(name + "_high", shape, F32R), sb(name + "_low", shape, F32R)

        HW = H // 2 + 2
        w_up = parts_of("w_up", [P, KT, H])
        w_full = parts_of("w_full", [P, HT, 2, HW])
        full_a = sb("full_a", [P, HT, 2, 2])
        w_down = parts_of("w_down", [P, HT, F])
        w_q, w_k, w_v = (parts_of(n, [P, KT, F]) for n in ("w_q", "w_k", "w_v"))
        w_o = sb("w_o", [P, KT, F])
        b_up = sb("b_up", [P, HT])
        b_down, b_q, b_k = (sb(n, [P, KT]) for n in ("b_down", "b_q", "b_k"))
        b_v, b_o, gamma_b, beta_b = (sb(n, [P, F]) for n in ("b_v", "b_o", "gamma_b", "beta_b"))
        mask_zero = sb("mask_zero", [P, T, NODES])
        mask_neg = sb("mask_neg", [P, T, NODES])
        masks = [mask_zero, mask_neg, mask_neg]
        ident = sb("ident", [P, P])
        minus_one = sb("minus_one", [P, 1])
        minus_half = sb("minus_half", [P, T])
        eps = sb("eps", [P, T])

        place = {}

        def lanes(name, shape):
            found = []
            for s in range(LANES):
                place[name, s] = (nc.sbuf_base + 31) // 32 * 32
                found.append(sb(f"{name}{s}", shape))
            return found

        def over(name, shape, host, skip=0):
            return [nc.alloc_sbuf_tensor_at(f"{name}{s}", shape, F32R, offset=place[host, s] + 4 * skip)
                    for s in range(LANES)]

        x_in = lanes("x_in", [P, T, F])
        x_cur = lanes("x_cur", [P, T, F])
        y_out = lanes("y_out", [P, T, F])
        norm = lanes("norm", [P, T, F])
        norm_t = lanes("norm_t", [P, KT, NODES])
        h_buf = lanes("h_buf", [P, T * max(H, F + 2)])
        hid_t = lanes("hid_t", [P, HT, NODES])
        low_t = lanes("low_t", [P, KT, NODES])
        probs = lanes("probs", [P, HEADS, T, NODES])
        probs_t = lanes("probs_t", [P, HEADS, T, NODES])
        stat = lanes("stat", [P, T, 6])
        mean_var = lanes("mean_var", [P, T, 2])
        var_eps = lanes("var_eps", [P, T])
        rstd = lanes("rstd", [P, T])
        full_f = lanes("full_f", [P, T, 2])
        top = lanes("top", [P, HEADS, T])
        neg_top = lanes("neg_top", [P, HEADS, T])
        shift = lanes("shift", [P, HEADS, T])
        sums = lanes("sums", [P, HEADS, T])
        inv = lanes("inv", [P, HEADS, T])
        out_stat = lanes("out_stat", [P, T, 6])
        out_mean_var = lanes("out_mean_var", [P, T, 2])
        out_var_eps = lanes("out_var_eps", [P, T])
        out_rstd = lanes("out_rstd", [P, T])
        h_gat = [b[:, 0:T * (F + 2)].rearrange("p (t f) -> p t f", t=T) for b in h_buf]
        vals = [b[:, 0:T * F].rearrange("p (t f) -> p t f", t=T) for b in h_buf]
        TILE = T * NODES
        norm_high = over("norm_high", [P, KT, NODES], "norm_t")
        norm_low = over("norm_low", [P, KT, NODES], "probs_t", 3 * TILE)
        h_full_high = over("h_full_high", [P, T, 2, H // 2], "h_buf")
        h_full_low = over("h_full_low", [P, T, 2, H // 2], "probs_t", 2 * TILE)
        probs_high = over("probs_high", [P, T, NODES], "probs_t")
        probs_low = over("probs_low", [P, T, NODES], "probs_t", TILE)
        hid_high = over("hid_high", [P, HT, NODES], "probs")
        hid_low = over("hid_low", [P, HT, NODES], "probs", 2 * TILE)
        q_high, q_low = over("q_high", [P, KT, NODES], "hid_t"), over("q_low", [P, KT, NODES], "hid_t", TILE)
        k_high, k_low = over("k_high", [P, KT, NODES], "h_buf", TILE), over("k_low", [P, KT, NODES], "low_t")
        att, att_t = norm, low_t
        pair = [ctx.enter_context(nc.psum_tensor(f"banks{s}", [P, 2, 512], F32)) for s in range(LANES)]
        banks = [[b[:, i, :] for i in range(2)] for b in pair]

        def wide_of(buf):
            return buf[:, :, :, :].rearrange("p h t n -> p (h t n)")

        stage_full = wide_of(probs[1])[:, 0:HT * H].rearrange("p (k f) -> p k f", k=HT)
        stage_up = wide_of(probs[2])[:, 0:KT * H].rearrange("p (k f) -> p k f", k=KT)
        stage_down = wide_of(probs[2])[:, KT * H:KT * H + HT * F].rearrange("p (k f) -> p k f", k=HT)
        stage_qkv = [probs[3][:, i, :, :] for i in range(3)]
        setup_adj = probs[0][:, 0, :, :].bitcast(I32)
        setup_a = wide_of(probs_t[0])
        setup_a_fc = wide_of(probs_t[1])
        setup_junk = wide_of(probs_t[2])

        def wide(ap):
            return ap[:, :, :].rearrange("p t f -> p (t f)")

        def pair_of(buf, i):
            return buf[:, 2 * i:2 * i + 2, :, :].rearrange("p h t n -> p (h t n)")

        s_weights, s_const, s_folded = sem("s_weights"), sem("s_const"), sem("s_folded")
        x_loaded, y_stored = sems("x_loaded", LANES), sems("y_stored", LANES)
        stats_made, var_ready, eps_added, rstd_ready, normed = (
            sems(n, 5) for n in ("stats_made", "var_ready", "eps_added", "rstd_ready", "normed"))
        turned, norm_t_ready = sems("turned", 4), sems("norm_t_ready", 4)
        h_mm, h_ready = sems("h_mm", 3), sems("h_ready", 3)
        spreaded, top_ready, neg_top_ready, scores_ready, leaky_ready, exps_ready, inv_ready, \
            probs_ready, probs_turned, probs_t_ready = (sems(n, 4) for n in (
                "spreaded", "top_ready", "neg_top_ready", "scores_ready", "leaky_ready", "exps_ready",
                "inv_ready", "probs_ready", "probs_turned", "probs_t_ready"))
        mixed, x_updated = sems("mixed", 3), sems("x_updated", 3)
        low_ready, exp_low_ready, elu_ready = (
            [None] + sems(n, 2) for n in ("low_ready", "exp_low_ready", "elu_ready"))
        exp_exp_ready, sum_ready = sem("exp_exp_ready"), sem("sum_ready")
        up_mm, hid_ready = sem("up_mm"), sem("hid_ready")
        norm_low_ready = {1: sem("norm_low_ready1"), 3: sem("norm_low_ready3")}
        hid_high_ready, hid_low_ready, hid_low_half = (
            sems(n, 2) for n in ("hid_high_ready", "hid_low_ready", "hid_low_half"))
        full_mm, full_ready, full_low_ready = (sems(n, 2) for n in ("full_mm", "full_ready", "full_low_ready"))
        probs_low_ready = sem("probs_low_ready")
        full_mixed, full_low, full_exp, full_exp_exp, full_elu, full_sum = (
            sem(n) for n in ("full_mixed", "full_low", "full_exp", "full_exp_exp", "full_elu", "full_sum"))
        down_mm, low_t_ready = sem("down_mm"), sem("low_t_ready")
        qk_mm, qk_high_ready = sems("qk_mm", 2), sems("qk_high_ready", 2)
        q_low_ready, v_mm, v_ready = (sem(n) for n in ("q_low_ready", "v_mm", "v_ready"))
        score_mm, head_top, head_shift, head_exps, head_turned, head_t_ready = (
            sems(n, HEADS // 2) for n in ("score_mm", "head_top", "head_shift", "head_exps", "head_turned",
                                          "head_t_ready"))
        av_mm, head_inv, att_ready, att_turned, att_t_ready = (
            sem(n) for n in ("av_mm", "head_inv", "att_ready", "att_turned", "att_t_ready"))
        wo_mm, out_pre_ready, scaled_ready, y_ready = (
            sem(n) for n in ("wo_mm", "out_pre_ready", "scaled_ready", "y_ready"))

        x_d = x.rearrange("b (p t) f -> b p t f", t=T)
        y_d = y.rearrange("b (p t) f -> b p t f", t=T)

        def rows(w):
            return w.rearrange("(k p) f -> p k f", p=P)

        def column(b):
            return b.rearrange("(k p) -> p k", p=P)

        def everywhere(v):
            return v.rearrange("(o f) -> o f", o=1).to_broadcast([P, v.shape[0]])

        WEIGHTS = [
            (w_gat[0][:, :, 0:F], rows(W0)), (w_gat[1][:, :, 0:F], rows(W_hand)), (w_gat[2][:, :, 0:F], rows(W2)),
            (stage_full, rows(W_fc)), (stage_up, rows(mlp1_w)), (stage_down, rows(mlp2_w)),
            (stage_qkv[0], rows(Wq)), (stage_qkv[1], rows(Wk)), (stage_qkv[2], rows(Wv)), (w_o[:, :, :], rows(Wo)),
            (setup_adj, adj.rearrange("(p t) j -> p t j", t=T)),
            (setup_a_fc[:, 0:2 * H], everywhere(a_fc.rearrange("f o -> (f o)"))),
            (b_up[:, :], column(mlp1_b)), (b_down[:, :], column(mlp2_b)), (b_q[:, :], column(bq)),
            (b_k[:, :], column(bk)),
            (b_v[:, :], everywhere(bv)), (b_o[:, :], everywhere(bo)), (gamma_b[:, :], everywhere(gamma)),
            (beta_b[:, :], everywhere(beta)),
        ] + [(setup_a[:, 2 * F * g:2 * F * (g + 1)], everywhere(a.rearrange("f o -> (f o)")))
             for g, a in enumerate((a0, a_hand, a2))]
        SPLITS = [(w_up[0][:, :, :], w_up[1][:, :, :], stage_up), (w_down[0][:, :, :], w_down[1][:, :, :], stage_down)]
        SPLITS += [(w[0][:, :, :], w[1][:, :, :], src) for w, src in zip((w_q, w_k, w_v), stage_qkv)]
        SPLITS += [(w_full[0][:, :, c, 0:F], w_full[1][:, :, c, 0:F], stage_full[:, :, c * F:(c + 1) * F])
                   for c in range(2)]
        SPLITS += [(w_full[0][:, :, c, F:HW], w_full[1][:, :, c, F:HW], full_a[:, :, c, :]) for c in range(2)]
        CONSTANTS = 5
        SETUP_STEPS = 1 + 6 * KT + 2 * HT + 2 * len(SPLITS)

        def run(eng, engine, steps):
            parts = timetable(engine)
            assert set(steps) == {step for _, step, i in parts}, engine
            for period in range(LANES):
                for lag, step, i in parts:
                    if lag <= period:
                        steps[step](i, period - lag, period - lag + 1, 16, None)
            with eng.Fori(0, ROUNDS - 1) as r:
                n_before = [eng.snap(r * LANES + (s + 1)) for s in range(LANES)]
                n_new = [eng.snap(r * LANES + (LANES + s + 1)) for s in range(LANES)]
                dma_before, dma_new = eng.snap(r * 16 + 16), eng.snap(r * 16 + 32)
                for v in n_before + n_new:
                    eng.to_reg(v)
                for period in range(LANES):
                    for lag, step, i in parts:
                        s = (period - lag) % LANES
                        if lag <= period:
                            steps[step](i, s, n_new[s], dma_new, n_before[s])
                        else:
                            steps[step](i, s, n_before[s], dma_before, None)
            for period in range(LANES):
                for lag, step, i in parts:
                    if lag > period:
                        s = (period - lag) % LANES
                        steps[step](i, s, SAMPLES - LANES + s + 1, 16 * ROUNDS, None)

        block = ctx.enter_context(nc.Block())

        @block.sync
        def _(sp):
            sp.dma_start(x_in[0][:, :, :], x_d[0]).then_inc(x_loaded[0], 16)
            with nc.allow_non_contiguous_dma(reason="four bias vectors, once"):
                for dst, src in WEIGHTS:
                    sp.dma_start(dst, src).then_inc(s_weights, 16)
            for s in range(LANES):
                sp.sem_inc(y_stored[s], 16)
            for s in range(1, LANES):
                sp.dma_start(x_in[s][:, :, :], x_d[s]).then_inc(x_loaded[s], 16)
            for s in range(LANES):
                sp.wait_ge(x_updated[0], s + 1)
                sp.dma_start(x_in[s][:, :, :], x_d[LANES + s]).then_inc(x_loaded[s], 16)
            with sp.Fori(0, ROUNDS - 2) as r:
                for s in range(LANES):
                    sp.wait_ge(x_updated[0], r * LANES + (LANES + s + 1))
                    sp.dma_start(x_in[s][:, :, :], x_d[r * LANES + (2 * LANES + s)]).then_inc(x_loaded[s], 16)
                    sp.wait_ge(y_ready, r * LANES + (s + 1))
                    sp.dma_start(y_d[r * LANES + s], y_out[s][:, :, :]).then_inc(y_stored[s], 16)
            for n in range((ROUNDS - 2) * LANES, SAMPLES):
                sp.wait_ge(y_ready, n + 1)
                sp.dma_start(y_d[n], y_out[n % LANES][:, :, :]).then_inc(y_stored[n % LANES], 16)
            for s in range(LANES):
                sp.wait_ge(y_stored[s], 16 * (ROUNDS + 1))

        @block.gpsimd
        def _(pool):
            pool.memset(ident[:, :], 0.0).then_inc(s_const, 1)
            pool.memset(minus_one[:, :], -1.0).then_inc(s_const, 1)
            pool.memset(minus_half[:, :], -0.5).then_inc(s_const, 1)
            pool.memset(eps[:, :], EPS).then_inc(s_const, 1)
            pool.wait_ge(s_const, 4)
            pool.affine_select(out=ident[:, :], in_=ident[:, :], compare_op=ALU.not_equal, fill=1.0, base=0,
                               pattern=[[-1, P]], channel_multiplier=1).then_inc(s_const, 1)
            pool.wait_ge(s_weights, 16 * len(WEIGHTS))

            def rstd_(l, s, n, dma, before):
                pool.wait_ge(var_ready[l], n)
                mv, ve, rs = (out_mean_var[s], out_var_eps[s], out_rstd[s]) if l == 4 else \
                    (mean_var[s], var_eps[s], rstd[s])
                pool.tensor_tensor(ve[:, :], mv[:, :, 1], eps[:, :], ALU.add).then_inc(eps_added[l], 1)
                pool.wait_ge(eps_added[l], n)
                pool.tensor_tensor(rs[:, :], ve[:, :], minus_half[:, :], ALU.pow)\
                    .then_inc(rstd_ready[l], 1)

            def finish(g, s, n, dma, before):
                if g == 3:
                    pool.wait_ge(full_elu, n)
                    pool.tensor_tensor(wide(hid_t[s]), wide(hid_t[s]), pair_of(probs_t[s], 1), ALU.add)\
                        .then_inc(full_sum, 1)
                else:
                    pool.wait_ge(elu_ready[2], n)
                    pool.tensor_tensor(x_cur[s][:, :, :], x_cur[s][:, :, :], probs[s][:, 1, :, :], ALU.add)\
                        .then_inc(x_updated[2], 1)

            def hid_low_(i, s, n, dma, before):
                pool.wait_ge(hid_high_ready[i], n)
                half = slice(0, HT // 2)
                pool.tensor_tensor(hid_low[s][:, half, :], hid_t[s][:, half, :], hid_high[s][:, half, :].bitcast(F32),
                                   ALU.subtract)\
                    .then_inc(hid_low_ready[i], 1)

            def beta_(_, s, n, dma, before):
                pool.wait_ge(normed[3], n)
                pool.tensor_tensor(x_cur[s][:, :, :], x_cur[s][:, :, :],
                                   beta_b[:, :].unsqueeze(1).to_broadcast([P, T, F]), ALU.add)

            def out(_, s, n, dma, before):
                pool.wait_ge(normed[4], n)
                pool.tensor_tensor(y_out[s][:, :, :], y_out[s][:, :, :],
                                   gamma_b[:, :].unsqueeze(1).to_broadcast([P, T, F]), ALU.mult)\
                    .then_inc(scaled_ready, 1)
                pool.wait_ge(scaled_ready, n)
                pool.tensor_tensor(y_out[s][:, :, :], y_out[s][:, :, :], x_cur[s][:, :, :], ALU.add)\
                    .then_inc(y_ready, 1)

            run(pool, POOL, {"rstd": rstd_, "hid_low": hid_low_, "finish": finish, "beta": beta_,
                             "out": out})

        @block.scalar
        def _(act):
            act.preload_act_table(ACT.Exp)
            act.wait_ge(s_const, CONSTANTS)
            act.wait_ge(s_weights, 16 * len(WEIGHTS))
            act.wait_ge(s_folded, SETUP_STEPS)

            def turn(l, s, n, dma, before):
                act.wait_ge(turned[l], n)
                dst = norm_t[s] if l in (0, 2) else norm_high[s]
                act.activation(wide(dst), banks[s][0][:, :], ACT.Relu).then_inc(norm_t_ready[l], 1)

            def up(_, s, n, dma, before):
                act.wait_ge(up_mm, n)
                for f in range(HT):
                    relu = act.activation(hid_t[s][:, f, :], banks[s][f // 2][:, (f % 2) * NODES:][:, 0:NODES],
                                          ACT.Relu, bias=b_up[:, f:f + 1])
                relu.then_inc(hid_ready, 1)

            def hid_high_(i, s, n, dma, before):
                act.wait_ge(hid_ready if i == 0 else full_sum, n)
                act.activation(wide(hid_high[s]), wide(hid_t[s]), ACT.Copy).then_inc(hid_high_ready[i], 1)

            def project(g, s, n, dma, before):
                act.wait_ge(h_mm[g], n)
                act.activation(h_gat[s], pair[s][:, :, 0:F + 2], ACT.Copy).then_inc(h_ready[g], 1)

            def biased(g, s, n, src, column_of):
                for t in range(T):
                    add = act.activation(probs[s][:, 0, t, :], src(t), ACT.Identity, bias=column_of(t))
                add.then_inc(scores_ready[g], 1)

            def add_f1(g, s, n, dma, before):
                act.wait_ge(top_ready[g], n)
                if g == 3:
                    biased(3, s, n, lambda t: banks[s][0][:, 0:NODES], lambda t: full_f[s][:, t, 0:1])
                else:
                    biased(g, s, n, lambda t: probs[s][:, 0, t, :], lambda t: h_gat[s][:, t, F:F + 1])

            def exps(g, s, n, dma, before):
                act.wait_ge(leaky_ready[g], n)
                for t in range(T):
                    ex = act.activation(probs[s][:, 0, t, :], probs[s][:, 0, t, :], ACT.Exp,
                                        bias=shift[s][:, 0, t:t + 1], accum_out=sums[s][:, 0, t:t + 1])
                ex.then_inc(exps_ready[g], 1)

            def turn_probs(g, s, n, dma, before):
                act.wait_ge(probs_turned[g], n)
                dst = probs_high[s] if g == 3 else probs_t[s][:, 0, :, :]
                act.activation(wide(dst), banks[s][1 if g == 3 else 0][:, :], ACT.Copy)\
                    .then_inc(probs_t_ready[g], 1)

            def mix(g, s, n, dma, before):
                if g == 3:
                    low = pair_of(probs[s], 1)
                    act.wait_ge(full_mixed, n)
                    act.activation(low, wide(pair[s]), ACT.Relu, scale=-1.0).then_inc(full_low, 1)
                    act.wait_ge(full_low, n)
                    act.activation(low, low, ACT.Exp, scale=-1.0).then_inc(full_exp, 1)
                    act.wait_ge(full_exp, n)
                    act.activation(low, low, ACT.Exp, bias=minus_one[:, 0:1]).then_inc(full_exp_exp, 1)
                    return
                low = wide(probs[s][:, 2, :, :])
                act.wait_ge(mixed[g], n)
                act.activation(low, banks[s][1][:, :], ACT.Relu, scale=-1.0).then_inc(low_ready[g], 1)
                act.wait_ge(low_ready[g], n)
                act.activation(low, low, ACT.Exp, scale=-1.0).then_inc(exp_low_ready[g], 1)
                if g == 1:
                    act.wait_ge(exp_low_ready[1], n)
                    act.activation(low, low, ACT.Exp, bias=minus_one[:, 0:1]).then_inc(exp_exp_ready, 1)

            def rows_(t, s, n, dma, before):
                act.wait_ge(full_mm[t], n)
                act.activation(h_full_high[s][:, t, :, :], pair[s][:, :, 0:H // 2], ACT.Copy).then_inc(full_ready[t], 1)

            def down(_, s, n, dma, before):
                act.wait_ge(down_mm, n)
                for f in range(KT):
                    relu = act.activation(low_t[s][:, f, :], banks[s][0][:, f * NODES:(f + 1) * NODES], ACT.Relu,
                                          bias=b_down[:, f:f + 1])
                relu.then_inc(low_t_ready, 1)

            def qk(i, s, n, dma, before):
                act.wait_ge(qk_mm[i], n)
                bank, b, high = ((1, b_q, q_high), (0, b_k, k_high))[i]
                for f in range(KT):
                    hi = act.activation(high[s][:, f, :], banks[s][bank][:, f * NODES:(f + 1) * NODES],
                                        ACT.Identity, bias=b[:, f:f + 1])
                hi.then_inc(qk_high_ready[i], 1)

            def scores(i, s, n, dma, before):
                act.wait_ge(head_shift[i], n)
                for h in (2 * i, 2 * i + 1):
                    for t in range(T):
                        ex = act.activation(probs[s][:, h, t, :], probs[s][:, h, t, :], ACT.Exp,
                                            bias=shift[s][:, h, t:t + 1], scale=SCALE,
                                            accum_out=sums[s][:, h, t:t + 1])
                ex.then_inc(head_exps[i], 1)

            def turn_heads(i, s, n, dma, before):
                act.wait_ge(head_turned[i], n)
                act.activation(pair_of(probs_t[s], i), wide(pair[s]), ACT.Copy).then_inc(head_t_ready[i], 1)

            def turn_out(_, s, n, dma, before):
                act.wait_ge(att_turned, n)
                act.activation(wide(att_t[s]), banks[s][1][:, :], ACT.Copy).then_inc(att_t_ready, 1)

            run(act, ACT_E, {"turn": turn, "up": up, "hid_high": hid_high_, "project": project, "add_f1": add_f1,
                             "exps": exps,
                             "turn_probs": turn_probs, "mix": mix, "rows": rows_, "down": down,
                             "qk": qk, "scores": scores,
                             "turn_heads": turn_heads, "turn_out": turn_out})

        @block.vector
        def _(dve):
            dve.wait_ge(s_weights, 16 * len(WEIGHTS))
            dve.wait_ge(s_const, CONSTANTS)
            by_tile = setup_adj.rearrange("p t (q u) -> p t u q", u=T)
            for t in range(T):
                for mask, test in ((mask_zero, ALU.is_equal), (mask_neg, ALU.is_le)):
                    dve.tensor_scalar(mask[:, t, :].rearrange("p (u q) -> p u q", u=T), by_tile[:, t], 0.0, MASKED,
                                      test, ALU.mult).then_inc(s_const, 1)
            dve.memset(full_a[:, :, :, :], 0.0).then_inc(s_folded, 1)
            steps = 1
            for g in range(3):
                for k in range(KT):
                    for half in range(2):
                        a = setup_a[:, (2 * g + half) * F:(2 * g + half + 1) * F]
                        dve.wait_ge(s_folded, steps)
                        dve.tensor_tensor_reduce(setup_junk[:, 0:F], w_gat[g][:, k, 0:F], a, 1.0, 0.0, ALU.mult,
                                                 ALU.add, w_gat[g][:, k, F + half:F + half + 1]).then_inc(s_folded, 1)
                        steps += 1
            for k in range(HT):
                for half in range(2):
                    dve.wait_ge(s_folded, steps)
                    dve.tensor_tensor_reduce(setup_junk[:, 0:H], stage_full[:, k, :],
                                             setup_a_fc[:, half * H:(half + 1) * H], 1.0, 0.0, ALU.mult, ALU.add,
                                             full_a[:, k, half, 0:1]).then_inc(s_folded, 1)
                    steps += 1
            for high, low, src in SPLITS:
                dve.wait_ge(s_folded, steps)
                dve.tensor_copy(high, src).then_inc(s_folded, 1)
                dve.wait_ge(s_folded, steps + 1)
                dve.tensor_tensor(low, src, high.bitcast(F32), ALU.subtract).then_inc(s_folded, 1)
                steps += 2
            assert steps == SETUP_STEPS
            dve.wait_ge(s_folded, steps)
            dve.wait_ge(s_const, CONSTANTS + 2 * T)

            def norm_low_(l, s, n, dma, before):
                dve.wait_ge(norm_t_ready[l], n)
                dve.scalar_tensor_tensor(out=wide(norm_low[s]), in0=banks[s][0][:, :], scalar=0.0,
                                         in1=wide(norm_high[s]).bitcast(F32), op0=ALU.max, op1=ALU.subtract)\
                    .then_inc(norm_low_ready[l], 1)

            def hid_low_(i, s, n, dma, before):
                dve.wait_ge(hid_high_ready[i], n)
                half = slice(HT // 2, HT)
                dve.tensor_tensor(hid_low[s][:, half, :], hid_t[s][:, half, :], hid_high[s][:, half, :].bitcast(F32),
                                  ALU.subtract).then_inc(hid_low_half[i], 1)

            def rows_low(t, s, n, dma, before):
                dve.wait_ge(full_ready[t], n)
                dve.tensor_copy(full_f[s][:, t, :], pair[s][:, :, H // 2])
                dve.tensor_tensor(h_full_low[s][:, t, :, :], pair[s][:, :, 0:H // 2],
                                  h_full_high[s][:, t, :, :].bitcast(F32), ALU.subtract).then_inc(full_low_ready[t], 1)

            def probs_low_(_, s, n, dma, before):
                dve.wait_ge(probs_t_ready[3], n)
                dve.tensor_tensor(wide(probs_low[s]), banks[s][1][:, :], wide(probs_high[s]).bitcast(F32),
                                  ALU.subtract).then_inc(probs_low_ready, 1)

            def qk_low(i, s, n, dma, before):
                dve.wait_ge(qk_high_ready[i], n)
                bank, b, high, low = ((1, b_q, q_high, q_low), (0, b_k, k_high, k_low))[i]
                for f in range(KT):
                    lo = dve.scalar_tensor_tensor(out=low[s][:, f, :],
                                                  in0=banks[s][bank][:, f * NODES:(f + 1) * NODES],
                                                  scalar=b[:, f:f + 1], in1=high[s][:, f, :].bitcast(F32),
                                                  op0=ALU.add, op1=ALU.subtract)
                if i == 0:
                    lo.then_inc(q_low_ready, 1)

            def normalise(l, s, n, dma, before):
                mv, rs = (out_mean_var[s], out_rstd[s]) if l == 4 else (mean_var[s], rstd[s])
                src, dst = [(x_in[s], norm[s]), (x_cur[s], norm[s]), (x_cur[s], norm[s]), (x_cur[s], norm[s]),
                            (y_out[s], y_out[s])][l]
                if l == 0 and before is not None:
                    dve.wait_ge(att_turned, before)
                dve.wait_ge(rstd_ready[l], n)
                for t in range(T):
                    nm = dve.tensor_scalar(dst[:, t, :], src[:, t, :], mv[:, t, 0:1], rs[:, t:t + 1],
                                           ALU.subtract, ALU.mult)
                nm.then_inc(normed[l], 1)

            def stats(l, s, n, dma, before):
                if l == 0:
                    dve.wait_ge(x_loaded[s], dma)
                elif l == 4:
                    dve.wait_ge(out_pre_ready, n)
                else:
                    dve.wait_ge(x_updated[l - 1], n)
                src = x_in[s] if l == 0 else y_out[s] if l == 4 else x_cur[s]
                st, mv = (out_stat[s], out_mean_var[s]) if l == 4 else (stat[s], mean_var[s])
                for t in range(T):
                    bn = dve.bn_stats(st[:, t, :], src[:, t, :])
                bn.then_inc(stats_made[l], 1)
                dve.wait_ge(s_const, CONSTANTS)
                dve.wait_ge(stats_made[l], n)
                for t in range(T):
                    ag = dve.bn_aggr(mv[:, t, :], st[:, t, :])
                ag.then_inc(var_ready[l], 1)

            def spread(g, s, n, dma, before):
                if g == 3:
                    dve.wait_ge(spreaded[3], n)
                    dve.tensor_reduce(top[s][:, 0, 0:1], banks[s][0][:, 0:NODES], AX.X, ALU.max)\
                        .then_inc(top_ready[3], 1)
                    dve.wait_ge(top_ready[3], n)
                    dve.tensor_scalar(neg_top[s][:, 0, :], full_f[s][:, :, 0], -1.0, top[s][:, 0, 0:1], ALU.mult,
                                      ALU.subtract).then_inc(neg_top_ready[3], 1)
                    dve.wait_ge(neg_top_ready[3], n)
                    dve.scalar_tensor_tensor(out=shift[s][:, 0, :], in0=neg_top[s][:, 0, :], scalar=FULL_SLOPE,
                                             in1=neg_top[s][:, 0, :], op0=ALU.mult, op1=ALU.min)
                    return
                dve.wait_ge(s_const, CONSTANTS)
                dve.wait_ge(spreaded[g], n)
                for t in range(T):
                    tt = dve.tensor_tensor_reduce(probs[s][:, 0, t, :], banks[s][1][:, 0:NODES], masks[g][:, t, :],
                                                  1.0, LEAST, ALU.add, ALU.max, top[s][:, 0, t:t + 1])
                tt.then_inc(top_ready[g], 1)
                dve.wait_ge(top_ready[g], n)
                dve.scalar_tensor_tensor(out=neg_top[s][:, 0, :], in0=top[s][:, 0, :], scalar=-1.0,
                                         in1=h_gat[s][:, :, F], op0=ALU.mult, op1=ALU.subtract)\
                    .then_inc(neg_top_ready[g], 1)
                dve.wait_ge(neg_top_ready[g], n)
                dve.scalar_tensor_tensor(out=shift[s][:, 0, :], in0=neg_top[s][:, 0, :], scalar=SLOPE[g],
                                         in1=neg_top[s][:, 0, :], op0=ALU.mult, op1=ALU.min)

            def leaky(g, s, n, dma, before):
                slope = (SLOPE + [FULL_SLOPE])[g]
                row = probs[s][:, 0, :, :].rearrange("p t n -> p (t n)")
                dve.wait_ge(scores_ready[g], n)
                dve.scalar_tensor_tensor(out=row, in0=row, scalar=slope, in1=row, op0=ALU.mult, op1=ALU.max)\
                    .then_inc(leaky_ready[g], 1)

            def divide(g, s, n, dma, before):
                dve.wait_ge(exps_ready[g], n)
                dve.reciprocal(inv[s][:, 0, :], sums[s][:, 0, :]).then_inc(inv_ready[g], 1)
                dve.wait_ge(inv_ready[g], n)
                for t in range(T):
                    pr = dve.tensor_scalar(probs[s][:, 0, t, :], probs[s][:, 0, t, :], inv[s][:, 0, t:t + 1], None,
                                           ALU.mult)
                pr.then_inc(probs_ready[g], 1)

            def mix(_, s, n, dma, before):
                dve.wait_ge(mixed[0], n)
                if before is not None:
                    dve.wait_ge(y_ready, before)
                dve.scalar_tensor_tensor(out=wide(x_cur[s]), in0=banks[s][1][:, :], scalar=0.0,
                                         in1=wide(x_in[s]), op0=ALU.max, op1=ALU.add).then_inc(x_updated[0], 1)

            def finish(g, s, n, dma, before):
                if g == 3:
                    dve.wait_ge(full_exp_exp, n)
                    dve.scalar_tensor_tensor(out=pair_of(probs_t[s], 1), in0=pair_of(probs[s], 1), scalar=-1.0,
                                             in1=wide(pair[s]), op0=ALU.add, op1=ALU.max).then_inc(full_elu, 1)
                    return
                dve.wait_ge(exp_exp_ready if g == 1 else exp_low_ready[2], n)
                dve.scalar_tensor_tensor(out=wide(probs[s][:, 1, :, :]), in0=wide(probs[s][:, 2, :, :]), scalar=-1.0,
                                         in1=banks[s][1][:, :], op0=ALU.add, op1=ALU.max).then_inc(elu_ready[g], 1)
                if g == 1:
                    dve.wait_ge(elu_ready[1], n)
                    dve.tensor_tensor(wide(probs[s][:, 1, :, :]), banks[s][0][:, :], wide(probs[s][:, 1, :, :]),
                                      ALU.add).then_inc(sum_ready, 1)
                    dve.wait_ge(sum_ready, n)
                    dve.scalar_tensor_tensor(out=wide(x_cur[s]), in0=wide(probs[s][:, 1, :, :]), scalar=0.0,
                                             in1=wide(x_cur[s]), op0=ALU.max, op1=ALU.add).then_inc(x_updated[1], 1)

            def values(_, s, n, dma, before):
                dve.wait_ge(v_mm, n)
                dve.tensor_tensor(vals[s], banks[s][1][:, :].rearrange("p (t f) -> p t f", t=T),
                                  b_v[:, :].unsqueeze(1).to_broadcast([P, T, F]), ALU.add).then_inc(v_ready, 1)

            def scores(i, s, n, dma, before):
                dve.wait_ge(s_const, CONSTANTS)
                dve.wait_ge(score_mm[i], n)
                for h in (2 * i, 2 * i + 1):
                    for t in range(T):
                        tt = dve.tensor_tensor_reduce(probs[s][:, h, t, :],
                                                      banks[s][h % 2][:, t * NODES:(t + 1) * NODES],
                                                      mask_zero[:, t, :], 1.0, LEAST, ALU.add, ALU.max,
                                                      top[s][:, h, t:t + 1])
                tt.then_inc(head_top[i], 1)
                dve.wait_ge(head_top[i], n)
                dve.tensor_scalar(shift[s][:, 2 * i:2 * i + 2, :], top[s][:, 2 * i:2 * i + 2, :], -SCALE, None,
                                  ALU.mult).then_inc(head_shift[i], 1)

            def mix_heads(_, s, n, dma, before):
                dve.wait_ge(head_exps[1], n)
                dve.reciprocal(inv[s][:, :, :], sums[s][:, :, :]).then_inc(head_inv, 1)
                dve.wait_ge(head_inv, n)
                dve.wait_ge(av_mm, n)
                dve.tensor_tensor(att[s][:, :, :].rearrange("p t (h d) -> p t h d", h=HEADS),
                                  banks[s][0][:, :].rearrange("p (t h d) -> p t h d", t=T, h=HEADS),
                                  inv[s][:, :, :].rearrange("p h t -> p t h").unsqueeze(3)
                                  .to_broadcast([P, T, HEADS, HD]), ALU.mult).then_inc(att_ready, 1)

            def out_project(_, s, n, dma, before):
                dve.wait_ge(y_stored[s], dma)
                dve.wait_ge(wo_mm, n)
                dve.tensor_tensor(y_out[s][:, :, :], banks[s][1][:, :].rearrange("p (t f) -> p t f", t=T),
                                  b_o[:, :].unsqueeze(1).to_broadcast([P, T, F]), ALU.add)\
                    .then_inc(out_pre_ready, 1)

            run(dve, DVE, {"stats": stats, "normalise": normalise, "spread": spread, "leaky": leaky, "divide": divide,
                           "mix": mix, "finish": finish, "norm_low": norm_low_, "qk_low": qk_low,
                           "hid_low": hid_low_, "rows_low": rows_low, "probs_low": probs_low_,
                           "values": values, "scores": scores, "mix_heads": mix_heads, "out_project": out_project})

        @block.tensor
        def _(pe):
            pe.wait_ge(s_const, CONSTANTS)
            pe.wait_ge(s_weights, 16 * len(WEIGHTS))
            pe.wait_ge(s_folded, SETUP_STEPS)

            ALL = slice(None)

            def product(out, lhs, rhs):
                for k, (a, b) in enumerate(zip(lhs, rhs)):
                    mm = pe.matmul(out, a, b, start=(k == 0), stop=(k == len(lhs) - 1))
                return mm

            def product_of_parts(out, lhs, rhs):
                for k, ((a, a_low), (b, b_low)) in enumerate(zip(lhs, rhs)):
                    pe.matmul(out, a, b, start=(k == 0), stop=False)
                    pe.matmul(out, a, b_low, start=False, stop=False)
                    mm = pe.matmul(out, a_low, b, start=False, stop=(k == len(lhs) - 1))
                return mm

            def of_both(parts, *index):
                return tuple(part[index] for part in parts)

            def turn_tiles(bank, src):
                for a in range(2):
                    for b in range(2):
                        tr = pe.transpose(bank[:, b * 2 * P + a * P:b * 2 * P + (a + 1) * P],
                                          src[:, a, b * P:(b + 1) * P], ident[:, :])
                return tr

            def tile(t):
                return slice(t * P, (t + 1) * P)

            def turn(l, s, n, dma, before):
                pe.wait_ge(normed[l], n)
                turn_tiles(banks[s][0], norm[s]).then_inc(turned[l], 1)

            def project(g, s, n, dma, before):
                src = low_t[s] if g == 1 else norm_t[s]
                if g == 0 and before is not None:
                    pe.wait_ge(out_pre_ready, before)
                pe.wait_ge(low_t_ready if g == 1 else norm_t_ready[[0, None, 2][g]], n)
                for t in range(T):
                    mm = product(banks[s][t][:, 0:F + 2], [src[:, k, tile(t)] for k in range(KT)],
                                 [w_gat[g][:, k, :] for k in range(KT)])
                mm.then_inc(h_mm[g], 1)

            def spread(g, s, n, dma, before):
                if g == 3:
                    pe.wait_ge(full_low_ready[1], n)
                    for t in range(T):
                        f2 = full_f[s][:, t, 1:2]
                        tr = pe.transpose(banks[s][0][:, tile(t)], f2.to_broadcast([P, P]), ident[:, :])
                    tr.then_inc(spreaded[3], 1)
                    return
                pe.wait_ge(h_ready[g], n)
                for t in range(T):
                    tr = pe.transpose(banks[s][1][:, tile(t)], h_gat[s][:, t, F + 1:F + 2].to_broadcast([P, P]),
                                      ident[:, :])
                tr.then_inc(spreaded[g], 1)

            def turn_probs(g, s, n, dma, before):
                pe.wait_ge(probs_ready[g], n)
                turn_tiles(banks[s][1 if g == 3 else 0], probs[s][:, 0, :, :]).then_inc(probs_turned[g], 1)

            def mix(g, s, n, dma, before):
                pe.wait_ge(probs_low_ready if g == 3 else probs_t_ready[g], n)
                if g == 3:
                    h_full, p_full = (h_full_high[s], h_full_low[s]), (probs_high[s], probs_low[s])
                    for half in range(2):
                        for f in range(2):
                            mm = product_of_parts(banks[s][half][:, f * NODES:(f + 1) * NODES],
                                                  [of_both(h_full, ALL, u, half, tile(f)) for u in range(T)],
                                                  [of_both(p_full, ALL, u, ALL) for u in range(T)])
                    mm.then_inc(full_mixed, 1)
                    return
                for t in range(T):
                    mm = product(banks[s][1][:, t * F:(t + 1) * F],
                                 [probs_t[s][:, 0, u, tile(t)] for u in range(T)],
                                 [h_gat[s][:, u, 0:F] for u in range(T)])
                if g == 1:
                    mm = turn_tiles(banks[s][0], low_t[s])
                mm.then_inc(mixed[g], 1)

            def up(_, s, n, dma, before):
                pe.wait_ge(norm_low_ready[1], n)
                norms = (norm_high[s], norm_low[s])
                for half in range(2):
                    for f in range(2):
                        mm = product_of_parts(banks[s][half][:, f * NODES:(f + 1) * NODES],
                                              [of_both(w_up, ALL, k, tile(2 * half + f)) for k in range(KT)],
                                              [of_both(norms, ALL, k, ALL) for k in range(KT)])
                mm.then_inc(up_mm, 1)

            def rows_(t, s, n, dma, before):
                if t == 0:
                    pe.wait_ge(hid_low_half[0], n)
                pe.wait_ge(hid_low_ready[0] if t == 0 else full_low_ready[0], n)
                hids = (hid_high[s], hid_low[s])
                for half in range(2):
                    mm = product_of_parts(banks[s][half][:, 0:HW],
                                          [of_both(hids, ALL, k, tile(t)) for k in range(HT)],
                                          [of_both(w_full, ALL, k, half, ALL) for k in range(HT)])
                mm.then_inc(full_mm[t], 1)

            def down(_, s, n, dma, before):
                pe.wait_ge(hid_low_half[1], n)
                pe.wait_ge(hid_low_ready[1], n)
                hids = (hid_high[s], hid_low[s])
                for f in range(KT):
                    mm = product_of_parts(banks[s][0][:, f * NODES:(f + 1) * NODES],
                                          [of_both(w_down, ALL, k, tile(f)) for k in range(HT)],
                                          [of_both(hids, ALL, k, ALL) for k in range(HT)])
                mm.then_inc(down_mm, 1)

            def qk(i, s, n, dma, before):
                if i == 0:
                    pe.wait_ge(norm_low_ready[3], n)
                norms = (norm_high[s], norm_low[s])
                bank, w = ((banks[s][1], w_q), (banks[s][0], w_k))[i]
                for f in range(KT):
                    mm = product_of_parts(bank[:, f * NODES:(f + 1) * NODES],
                                          [of_both(w, ALL, k, tile(f)) for k in range(KT)],
                                          [of_both(norms, ALL, k, ALL) for k in range(KT)])
                mm.then_inc(qk_mm[i], 1)

            def values(_, s, n, dma, before):
                pe.wait_ge(q_low_ready, n)
                norms = (norm_high[s], norm_low[s])
                for t in range(T):
                    mm = product_of_parts(banks[s][1][:, t * F:(t + 1) * F],
                                          [of_both(norms, ALL, k, tile(t)) for k in range(KT)],
                                          [of_both(w_v, ALL, k, ALL) for k in range(KT)])
                mm.then_inc(v_mm, 1)

            def scores(i, s, n, dma, before):
                pe.wait_ge(v_ready, n)
                if i == 1:
                    pe.wait_ge(head_top[0], n)
                for h in (2 * i, 2 * i + 1):
                    d = slice((h % 2) * HD, (h % 2 + 1) * HD)
                    for t in range(T):
                        mm = product_of_parts(banks[s][h % 2][:, t * NODES:(t + 1) * NODES],
                                              [of_both((q_high[s], q_low[s]), d, h // 2, tile(t))],
                                              [of_both((k_high[s], k_low[s]), d, h // 2, ALL)])
                mm.then_inc(score_mm[i], 1)

            def turn_heads(i, s, n, dma, before):
                pe.wait_ge(head_exps[i], n)
                pe.wait_ge([head_top[1], head_t_ready[0]][i], n)
                for h in (2 * i, 2 * i + 1):
                    tr = turn_tiles(banks[s][h % 2], probs[s][:, h, :, :])
                tr.then_inc(head_turned[i], 1)

            def mix_heads(_, s, n, dma, before):
                for i in range(HEADS // 2):
                    pe.wait_ge(head_t_ready[i], n)
                for t in range(T):
                    for h in range(HEADS):
                        mm = product(banks[s][0][:, t * F + h * HD:t * F + (h + 1) * HD],
                                     [probs_t[s][:, h, u, tile(t)] for u in range(T)],
                                     [vals[s][:, u, h * HD:(h + 1) * HD] for u in range(T)])
                mm.then_inc(av_mm, 1)

            def turn_out(_, s, n, dma, before):
                pe.wait_ge(att_ready, n)
                turn_tiles(banks[s][1], att[s]).then_inc(att_turned, 1)

            def out_project(_, s, n, dma, before):
                pe.wait_ge(att_t_ready, n)
                for t in range(T):
                    mm = product(banks[s][1][:, t * F:(t + 1) * F], [att_t[s][:, k, tile(t)] for k in range(KT)],
                                 [w_o[:, k, :] for k in range(KT)])
                mm.then_inc(wo_mm, 1)

            run(pe, PE, {"turn": turn, "project": project, "spread": spread, "turn_probs": turn_probs, "mix": mix,
                         "up": up, "rows": rows_, "down": down, "qk": qk,
                         "values": values, "scores": scores, "turn_heads": turn_heads, "mix_heads": mix_heads,
                         "turn_out": turn_out, "out_project": out_project})


_INS = ["x", "adj", "L0_gnn_W", "L0_gnn_a", "L1_gnn_mlp1_w", "L1_gnn_mlp1_b", "L1_gnn_mlp2_w", "L1_gnn_mlp2_b",
        "L1_gnn_W_fc", "L1_gnn_a_fc", "L1_gnn_W_hand", "L1_gnn_a_hand", "L2_gnn_W", "L2_gnn_a", "L3_gnn_Wq",
        "L3_gnn_bq", "L3_gnn_Wk", "L3_gnn_bk", "L3_gnn_Wv", "L3_gnn_bv", "L3_gnn_Wo", "L3_gnn_bo",
        "L3_gnn_gamma", "L3_gnn_beta"]


def kernel(**inputs):
    import numpy as np
    import concourse.bacc as bacc
    from concourse import mybir
    from concourse.bass_utils import run_bass_kernel_spmd

    nc = bacc.Bacc("TRN2", target_bir_lowering=False, num_devices=1)
    arrays, args = {}, []
    for name in _INS:
        a = np.ascontiguousarray(inputs[name])
        arrays[f"in_{name}_dram"] = a
        args.append(nc.dram_tensor(f"in_{name}_dram", a.shape, mybir.dt.from_np(a.dtype), kind="ExternalInput").ap())
    args.append(nc.dram_tensor("out_0_dram", inputs["x"].shape, mybir.dt.float32, kind="ExternalOutput").ap())
    bass_graph_layers(nc, *args)
    r = run_bass_kernel_spmd(nc, [arrays], core_ids=[0])
    return r.results[0]["out_0_dram"]
```
